# Optimizing a Trainium2 kernel written in Bass

```python
import numpy as np
import jax
import jax.numpy as jnp

def _softmax(x, axis=-1):
    return jax.nn.softmax(x, axis=axis)

def _gelu(x):
    return jax.nn.gelu(x, approximate=True)

def _silu(x):
    return jax.nn.silu(x)

def _sigmoid(x):
    return jax.nn.sigmoid(x)

def _layernorm(x, axis=-1, eps=1e-05):
    m = jnp.mean(x, axis=axis, keepdims=True)
    v = jnp.var(x, axis=axis, keepdims=True)
    return (x - m) / jnp.sqrt(v + eps)

def _scatter_add(tgt, idx, src, axis=0):
    return tgt.at[idx].add(src)

def _segment_sum(src, seg, n):
    return jax.ops.segment_sum(src, seg, n)
kernel_name = 'mk_cond_seq_d2_seqx_r8_4e81e3'

def setup_inputs(seed: int=0):
    np.random.seed(seed)
    _w = jnp.asarray

    def _rec_inputs():
        import jax
        import jax.numpy as jnp
        _rk = jax.random.key(seed)
        x = 1.648e-05 + 1 * jax.random.normal(jax.random.fold_in(_rk, 1), (2, 512, 144), jnp.float32)
        _lenS = 512 - jax.random.randint(jax.random.fold_in(_rk, 7), (2,), 0, max(1, 512 // 4) + 1, jnp.int32)
        _lenS2 = 512 - jax.random.randint(jax.random.fold_in(_rk, 8), (2,), 0, max(1, 512 // 4) + 1, jnp.int32)
        cond_1152 = 0.00914911 + 1.00357 * jax.random.normal(jax.random.fold_in(_rk, 11), (2, 144), jnp.float32)
        return (x, cond_1152)
    x, cond_1152 = _rec_inputs()

    def _L0_cond_setup():
        import jax, jax.numpy as jnp
        import numpy as np
        NUM_HEADS = 16
        NUM_EXPERTS = 4
        TOP_K = 2
        LN_EPS = 1e-06

        def _ln(h):
            mu = jnp.mean(h, axis=-1, keepdims=True)
            var = jnp.var(h, axis=-1, keepdims=True)
            return (h - mu) * jax.lax.rsqrt(var + LN_EPS)

        def _modulate(h, shift, scale):
            return h * (1.0 + scale[:, None, :]) + shift[:, None, :]
        key = jax.random.key(seed)
        ks = jax.random.split(key, 12)
        B, N, C = (8, 128, 144)
        H = 4 * C
        E = NUM_EXPERTS
        s = 0.02
        return {'x': jax.random.normal(ks[0], (B, N, C), jnp.float32), 'c': jax.random.normal(ks[1], (B, C), jnp.float32), 'w_adaln': jax.random.normal(ks[2], (C, 6 * C), jnp.float32) * s, 'b_adaln': jnp.zeros((6 * C,), jnp.float32), 'w_qkv': jax.random.normal(ks[3], (C, 3 * C), jnp.float32) * s, 'b_qkv': jnp.zeros((3 * C,), jnp.float32), 'w_proj': jax.random.normal(ks[4], (C, C), jnp.float32) * s, 'b_proj': jnp.zeros((C,), jnp.float32), 'w_gate': jax.random.normal(ks[5], (C, E), jnp.float32) * s, 'w1': jax.random.normal(ks[6], (E, C, H), jnp.float32) * s, 'b1': jnp.zeros((E, H), jnp.float32), 'w2': jax.random.normal(ks[7], (E, H, C), jnp.float32) * s, 'b2': jnp.zeros((E, C), jnp.float32)}
    _L0_cond_all = _L0_cond_setup()
    _L0_cond_in = {k: v for k, v in _L0_cond_all.items() if k in ('w_adaln', 'b_adaln', 'w_qkv', 'b_qkv', 'w_proj', 'b_proj', 'w_gate', 'w1', 'b1', 'w2', 'b2')}
    del _L0_cond_all

    def _L1_cond_setup():
        import jax, jax.numpy as jnp
        import numpy as np
        B, N, D = (8, 128, 144)
        H = 16
        HD = D // H
        HID = 4 * D
        EPS = 1e-06

        def _ln(x):
            mu = jnp.mean(x, axis=-1, keepdims=True)
            var = jnp.mean(jnp.square(x - mu), axis=-1, keepdims=True)
            return (x - mu) * jax.lax.rsqrt(var + EPS)

        def _modulate(x, shift, scale):
            return x * (1.0 + scale[:, None, :]) + shift[:, None, :]

        def _attn(x, w_qkv, b_qkv, w_proj, b_proj):
            b, n, d = x.shape
            qkv = (x @ w_qkv + b_qkv).reshape(b, n, 3, H, HD)
            q = qkv[:, :, 0].transpose(0, 2, 1, 3)
            k = qkv[:, :, 1].transpose(0, 2, 1, 3)
            v = qkv[:, :, 2].transpose(0, 2, 1, 3)
            scores = jnp.einsum('bhnd,bhmd->bhnm', q, k) * HD ** (-0.5)
            attn = jax.nn.softmax(scores, axis=-1)
            out = jnp.einsum('bhnm,bhmd->bhnd', attn, v)
            out = out.transpose(0, 2, 1, 3).reshape(b, n, d)
            return out @ w_proj + b_proj
        key = jax.random.key(seed)
        ks = jax.random.split(key, 12)
        s = 0.02
        return {'x': jax.random.normal(ks[0], (B, N, D), jnp.float32), 't_emb': jax.random.normal(ks[1], (B, D), jnp.float32), 'w_qkv': jax.random.normal(ks[2], (D, 3 * D), jnp.float32) * s, 'b_qkv': jax.random.normal(ks[3], (3 * D,), jnp.float32) * s, 'w_proj': jax.random.normal(ks[4], (D, D), jnp.float32) * s, 'b_proj': jax.random.normal(ks[5], (D,), jnp.float32) * s, 'w_fc1': jax.random.normal(ks[6], (D, HID), jnp.float32) * s, 'b_fc1': jax.random.normal(ks[7], (HID,), jnp.float32) * s, 'w_fc2': jax.random.normal(ks[8], (HID, D), jnp.float32) * s, 'b_fc2': jax.random.normal(ks[9], (D,), jnp.float32) * s, 'w_ada': jax.random.normal(ks[10], (D, 6 * D), jnp.float32) * s, 'b_ada': jax.random.normal(ks[11], (6 * D,), jnp.float32) * s}
    _L1_cond_all = _L1_cond_setup()
    _L1_cond_in = {k: v for k, v in _L1_cond_all.items() if k in ('w_qkv', 'b_qkv', 'w_proj', 'b_proj', 'w_fc1', 'b_fc1', 'w_fc2', 'b_fc2', 'w_ada', 'b_ada')}
    del _L1_cond_all
    return {'x': x, 'cond_1152': cond_1152, 'L0_cond_w_adaln': _L0_cond_in['w_adaln'], 'L0_cond_b_adaln': _L0_cond_in['b_adaln'], 'L0_cond_w_qkv': _L0_cond_in['w_qkv'], 'L0_cond_b_qkv': _L0_cond_in['b_qkv'], 'L0_cond_w_proj': _L0_cond_in['w_proj'], 'L0_cond_b_proj': _L0_cond_in['b_proj'], 'L0_cond_w_gate': _L0_cond_in['w_gate'], 'L0_cond_w1': _L0_cond_in['w1'], 'L0_cond_b1': _L0_cond_in['b1'], 'L0_cond_w2': _L0_cond_in['w2'], 'L0_cond_b2': _L0_cond_in['b2'], 'L1_cond_w_qkv': _L1_cond_in['w_qkv'], 'L1_cond_b_qkv': _L1_cond_in['b_qkv'], 'L1_cond_w_proj': _L1_cond_in['w_proj'], 'L1_cond_b_proj': _L1_cond_in['b_proj'], 'L1_cond_w_fc1': _L1_cond_in['w_fc1'], 'L1_cond_b_fc1': _L1_cond_in['b_fc1'], 'L1_cond_w_fc2': _L1_cond_in['w_fc2'], 'L1_cond_b_fc2': _L1_cond_in['b_fc2'], 'L1_cond_w_ada': _L1_cond_in['w_ada'], 'L1_cond_b_ada': _L1_cond_in['b_ada']}

def reference(x, cond_1152, L0_cond_w_adaln, L0_cond_b_adaln, L0_cond_w_qkv, L0_cond_b_qkv, L0_cond_w_proj, L0_cond_b_proj, L0_cond_w_gate, L0_cond_w1, L0_cond_b1, L0_cond_w2, L0_cond_b2, L1_cond_w_qkv, L1_cond_b_qkv, L1_cond_w_proj, L1_cond_b_proj, L1_cond_w_fc1, L1_cond_b_fc1, L1_cond_w_fc2, L1_cond_b_fc2, L1_cond_w_ada, L1_cond_b_ada):
    import jax
    import jax.numpy as jnp

    def _L0_cond_ref(x, c, w_adaln, b_adaln, w_qkv, b_qkv, w_proj, b_proj, w_gate, w1, b1, w2, b2):
        import jax, jax.numpy as jnp
        import numpy as np
        NUM_HEADS = 16
        NUM_EXPERTS = 4
        TOP_K = 2
        LN_EPS = 1e-06

        def _ln(h):
            mu = jnp.mean(h, axis=-1, keepdims=True)
            var = jnp.var(h, axis=-1, keepdims=True)
            return (h - mu) * jax.lax.rsqrt(var + LN_EPS)

        def _modulate(h, shift, scale):
            return h * (1.0 + scale[:, None, :]) + shift[:, None, :]
        B, N, C = x.shape
        nh = NUM_HEADS
        hd = C // nh
        mod = jax.nn.silu(c) @ w_adaln + b_adaln
        sh_msa, sc_msa, g_msa, sh_mlp, sc_mlp, g_mlp = jnp.split(mod, 6, axis=-1)
        h = _modulate(_ln(x), sh_msa, sc_msa)
        qkv = (h @ w_qkv + b_qkv).reshape(B, N, 3, nh, hd).transpose(2, 0, 3, 1, 4)
        q, k, v = (qkv[0], qkv[1], qkv[2])
        attn = jax.nn.softmax(jnp.einsum('bhqd,bhkd->bhqk', q, k) * hd ** (-0.5), axis=-1)
        o = jnp.einsum('bhqk,bhkd->bhqd', attn, v).transpose(0, 2, 1, 3).reshape(B, N, C)
        o = o @ w_proj + b_proj
        x = x + g_msa[:, None, :] * o
        xn = _modulate(_ln(x), sh_mlp, sc_mlp)
        xf = xn.reshape(-1, C)
        gate_logits = xf @ w_gate
        topk_logits, topk_idx = jax.lax.top_k(gate_logits, TOP_K)
        gates = jax.nn.softmax(topk_logits, axis=-1)
        cw = jnp.sum(jax.nn.one_hot(topk_idx, NUM_EXPERTS, dtype=xf.dtype) * gates[..., None], axis=1)
        hmid = jax.nn.gelu(jnp.einsum('tc,ech->eth', xf, w1) + b1[:, None, :], approximate=True)
        eo = jnp.einsum('eth,ehc->etc', hmid, w2) + b2[:, None, :]
        moe = jnp.einsum('te,etc->tc', cw, eo).reshape(B, N, C)
        return x + g_mlp[:, None, :] * moe

    def _L1_cond_ref(x, t_emb, w_qkv, b_qkv, w_proj, b_proj, w_fc1, b_fc1, w_fc2, b_fc2, w_ada, b_ada):
        import jax, jax.numpy as jnp
        import numpy as np
        B, N, D = (8, 128, 144)
        H = 16
        HD = D // H
        HID = 4 * D
        EPS = 1e-06

        def _ln(x):
            mu = jnp.mean(x, axis=-1, keepdims=True)
            var = jnp.mean(jnp.square(x - mu), axis=-1, keepdims=True)
            return (x - mu) * jax.lax.rsqrt(var + EPS)

        def _modulate(x, shift, scale):
            return x * (1.0 + scale[:, None, :]) + shift[:, None, :]

        def _attn(x, w_qkv, b_qkv, w_proj, b_proj):
            b, n, d = x.shape
            qkv = (x @ w_qkv + b_qkv).reshape(b, n, 3, H, HD)
            q = qkv[:, :, 0].transpose(0, 2, 1, 3)
            k = qkv[:, :, 1].transpose(0, 2, 1, 3)
            v = qkv[:, :, 2].transpose(0, 2, 1, 3)
            scores = jnp.einsum('bhnd,bhmd->bhnm', q, k) * HD ** (-0.5)
            attn = jax.nn.softmax(scores, axis=-1)
            out = jnp.einsum('bhnm,bhmd->bhnd', attn, v)
            out = out.transpose(0, 2, 1, 3).reshape(b, n, d)
            return out @ w_proj + b_proj
        ada = jax.nn.silu(t_emb) @ w_ada + b_ada
        shift_a, scale_a, gate_a, shift_f, scale_f, gate_f = jnp.split(ada, 6, axis=-1)
        x = x + gate_a[:, None, :] * _attn(_modulate(_ln(x), shift_a, scale_a), w_qkv, b_qkv, w_proj, b_proj)
        h = _modulate(_ln(x), shift_f, scale_f)
        h = jax.nn.gelu(h @ w_fc1 + b_fc1, approximate=True) @ w_fc2 + b_fc2
        return x + gate_f[:, None, :] * h
    x = _L0_cond_ref(x, cond_1152, L0_cond_w_adaln, L0_cond_b_adaln, L0_cond_w_qkv, L0_cond_b_qkv, L0_cond_w_proj, L0_cond_b_proj, L0_cond_w_gate, L0_cond_w1, L0_cond_b1, L0_cond_w2, L0_cond_b2)
    x = _L1_cond_ref(x, cond_1152, L1_cond_w_qkv, L1_cond_b_qkv, L1_cond_w_proj, L1_cond_b_proj, L1_cond_w_fc1, L1_cond_b_fc1, L1_cond_w_fc2, L1_cond_b_fc2, L1_cond_w_ada, L1_cond_b_ada)
    return x

_drawn_inputs = setup_inputs


def setup_inputs(seed=0):
    import zlib

    import numpy as np

    out = dict(_drawn_inputs(seed))
    spreads = {'L0_cond_b_adaln': (0.0, 0.543),
     'L0_cond_b_qkv': (0.0, 0.8),
     'L0_cond_b_proj': (0.0, 0.436),
     'L0_cond_b1': (0.0, 0.8),
     'L0_cond_b2': (0.0, 0.707)}
    factors = {'cond_1152': 2.848,
     'L0_cond_w_adaln': 3.024,
     'L0_cond_w_qkv': 8.0,
     'L0_cond_w_proj': 8.0,
     'L0_cond_w_gate': 5.685,
     'L0_cond_w1': 7.248,
     'L0_cond_w2': 6.61,
     'L1_cond_w_qkv': 8.0,
     'L1_cond_b_qkv': 8.0,
     'L1_cond_w_proj': 8.0,
     'L1_cond_b_proj': 57.674,
     'L1_cond_w_fc1': 6.724,
     'L1_cond_b_fc1': 26.282,
     'L1_cond_w_fc2': 6.51,
     'L1_cond_b_fc2': 63.759,
     'L1_cond_w_ada': 5.663,
     'L1_cond_b_ada': 8.0}
    for name, (base, spread) in spreads.items():
        noise = np.random.default_rng([zlib.crc32(name.encode()), seed]).standard_normal(out[name].shape)
        drawn = base * np.exp(spread * noise) if base else spread * noise
        out[name] = jnp.asarray(drawn.astype(out[name].dtype))
    for name, factor in factors.items():
        out[name] = (out[name] * factor).astype(out[name].dtype)
    return out
```

```python
from contextlib import ExitStack

import concourse.bass as bass
from concourse import mybir

F32 = mybir.dt.float32
BF16 = mybir.dt.bfloat16
I32 = mybir.dt.int32
ALU = mybir.AluOpType
ACT = mybir.ActivationFunctionType
AX = mybir.AxisListType

P = 128
B, N, C = 2, 512, 144
NT = N // P
NH, HD = 16, 9
CR = C - P
E, HID = 4, 4 * C
CH = E * HID // P
CH1 = -(-HID // P)
L = 2
EPS = 1e-6
SCALE = HD ** -0.5
PARTS = 3
PAIRS = PARTS * PARTS * HD
MROW = 96
SROWS = MROW + PARTS
G = 4
HG = NH // G
UNIT_LEAD = 6
OW = 32

STACK = {0: ((0, 2), (16, 1), (32, 0)), 1: ((49, 1), (65, 0)), 2: ((82, 0),)}
BIAS_ROWS = (48, 81, 98)
ROWS = 99
MASK1, MASK2 = 49, 82

WCOLS = {}
_at = 0
for _name, _n in (("qkv0", 3 * C), ("proj0", C), ("gate", E), ("w1", E * HID),
                  ("qkv1", 3 * C), ("proj1", C), ("fc1", HID)):
    WCOLS[_name] = (_at, _n)
    _at += _n
WN = _at


def schedule():
    s = [("ada", 0), ("ln", 0, 0), ("turn", 0, 0, "a"), ("qkv", 0, 0), ("ada", 1)]
    s += [("ln", 0, 1), ("turn", 0, 1, "a"), ("qkv", 0, 1), ("wsplit",)]
    for l in range(L):
        n0 = B * l
        if l:
            s += [("turn", l, 1, "a"), ("qkv", l, 1)]
        s += [("max", n0, u) for u in range(UNIT_LEAD)]
        for g in range(B * HG):
            s += [("slot", n0, g, k) for k in range(NT)]
            if g == 4:
                s += [("osplit", l, 0), ("turn", l, 0, "a"), ("proj", l, 0), ("ln", l, 2)]
            if g == 6:
                s += [("turn", l, 0, "b")] + [("gate", 0)] * (l == 0)
        s += [("tail", n0, k) for k in range(3)]
        s += [("osplit", l, 1), ("turn", l, 1, "a"), ("proj", l, 1), ("ln", l, 3)]
        half = CH // 2
        if l == 0:
            s += [("fc1", 0, 0), ("turn", l, 1, "b"), ("gate", 1), ("fc2", 0, 0), ("fc1", 0, 1), ("fc2", 0, 1)]
            s += [("ln", 1, 0), ("fc1", 1, 0), ("turn", 1, 0, "a"), ("qkv", 1, 0), ("fc2", 1, 0),
                  ("fc1", 1, 1), ("fc2", 1, 1), ("ln", 1, 1)]
        else:
            s += [("mlp1", 0), ("turn", l, 1, "b"), ("mlp2", 0), ("mlp1", 1), ("mlp2", 1)]
    return s


SCHED = schedule()
E2 = E // 2
CHH = CH // 2


def unit_of(stage):
    u = stage[2] if stage[0] == "max" else NT * stage[2] + stage[3] + UNIT_LEAD if stage[0] == "slot" else None
    return u if u is not None and u < B * NH else None


def finishes(stage):
    if stage[0] == "slot" and stage[2]:
        return stage[2] - 1, stage[3]
    if stage[0] == "tail":
        return B * HG - 1, stage[2]
    return None, None


def banks_used(stage):
    kind, s, t = stage[0], 0, 0
    if kind == "ada":
        t = 2 * B
    elif kind == "turn":
        t = 2
    elif kind == "qkv":
        t = 3 + NT // 2
    elif kind == "proj":
        s = NT // 2
    elif kind == "gate":
        s = 1
    elif kind == "fc1":
        t = CHH
    elif kind == "fc2":
        s = NT * E2
    elif kind == "mlp1":
        t = CH1
    elif kind == "mlp2":
        s = NT
    if kind == "slot":
        t += G
    u = unit_of(stage)
    if u is not None:
        s += NT
        t += u % 2
    if finishes(stage)[1] == 2:
        s += 1
    return s, t


S_AT, T_AT = [0], [0]
for _stage in SCHED:
    _s, _t = banks_used(_stage)
    S_AT.append(S_AT[-1] + _s)
    T_AT.append(T_AT[-1] + _t)
WHERE = {}
for _i, _stage in enumerate(SCHED):
    WHERE[_stage] = _i


PAIR_STAGE = [i for i, stage in enumerate(SCHED) if unit_of(stage) is not None and unit_of(stage) % 2]


def pair_turned(pair):
    return T_AT[PAIR_STAGE[pair] + 1]


def tile_used(i):
    _, l, b, buf = SCHED[i]
    if buf == "b":
        return max(j for j, s in enumerate(SCHED)
                   if j > i and (s[:2] == ("fc1", b) if l == 0 else s == ("mlp1", b)))
    return min(j for j, s in enumerate(SCHED) if j > i and s[0] in ("qkv", "proj"))


BACK_STAGE = [i for i, stage in enumerate(SCHED) if finishes(stage)[1] == 2]


def turned_back(gn):
    return S_AT[BACK_STAGE[gn] + 1]


def scores_ended(n):
    n0, b = n - n % B, n % B
    return T_AT[WHERE[("slot", n0, HG * (b + 1) - 1, NT - 1)]] + G


def hidden_parts(e):
    lo, parts = (e % E2) * HID, []
    while lo < (e % E2 + 1) * HID:
        hi = min((lo // P + 1) * P, (e % E2 + 1) * HID)
        parts.append((lo // P, lo % P, lo % P + hi - lo))
        lo = hi
    return parts


def build(nc, t, out):
    ctx = ExitStack()
    with ctx:
        def sb(name, shape, dt=F32):
            return ctx.enter_context(nc.sbuf_tensor(name, shape, dt))

        def sem(name):
            return ctx.enter_context(nc.semaphore(name))

        banks = [ctx.enter_context(nc.psum_tensor(f"bank{i}", [P, 512], F32)) for i in range(8)]
        S_BANKS, T_BANKS, O_BANKS = banks[0:3], banks[3:6], banks[6:8]
        NS, NTB = len(S_BANKS), len(T_BANKS)

        qk_dram = nc.dram_tensor("qk_parts", (B * L, 2, PARTS, HD * NH, N), BF16, kind="Internal").ap()
        m_dram = nc.dram_tensor("maxima", (B * L * NH // 2, PARTS, 2 * NT, P), BF16, kind="Internal").ap()

        ident = sb("ident", [P, P])
        identb = sb("identb", [P, P], BF16)
        ones = sb("ones", [P, P])
        mask1 = sb("mask1", [P, 1])
        mask2 = sb("mask2", [P, 1])
        before = sb("before", [P, E, E])
        wqkv = [sb(f"wqkv{l}", [P, 3 * C]) for l in range(L)]
        wqk = [sb(f"wqk{l}", [P, 2 * C]) for l in range(L)]
        wqk_stk = [sb(f"wqk_stk{l}", [ROWS, 2 * C], BF16) for l in range(L)]
        wproj = [sb(f"wproj{l}", [P, C]) for l in range(L)]
        wgate = sb("wgate", [P, E])
        w1 = sb("w1", [P, E * HID])
        w2 = sb("w2", [P, CH * C])
        wfc1 = sb("wfc1", [P, HID])
        wfc2 = sb("wfc2", [P, CH1, C])
        wstk = sb("wstk", [ROWS, WN], BF16)
        b2bc = sb("b2bc", [P, E, C])
        bfc2 = sb("bfc2", [P, C])
        wada = [w1[:, l * 6 * C:(l + 1) * 6 * C] for l in range(L)]
        wadar = [w2[0:CR + 1, l * 6 * C:(l + 1) * 6 * C] for l in range(L)]
        cT = sb("cT", [P, B])
        cTr = sb("cTr", [CR, B])
        ex = sb("ex", [P, B])
        exr = sb("exr", [CR, B])
        siluB = sb("siluB", [P, B, P])
        siluBr = sb("siluBr", [CR + 1, B, P])
        mod = [sb(f"mod{l}", [P, B, 6, C]) for l in range(L)]
        x = sb("x", [P, B, NT, C])
        hN = sb("hN", [P, NT, C])
        stN = sb("stN", [P, NT, 100], BF16)
        rest = sb("rest", [P, NT, CR])
        oN = [sb(f"oN{b}", [P, NT, C]) for b in range(B)]
        hT = {"a": [sb("hTa", [P, N])] * B, "b": [sb(f"hTb{b}", [P, N]) for b in range(B)]}
        hS = {"a": [sb("hSa", [ROWS, N], BF16)] * B, "b": [sb(f"hSb{b}", [ROWS, N], BF16) for b in range(B)]}
        Qs = [sb(f"Qs{b}", [P, NH, N], BF16) for b in range(B)]
        Ks = [sb(f"Ks{b}", [P, NH, N], BF16) for b in range(B)]
        Va = [sb(f"Va{b}", [P, NT, NH, OW]) for b in range(B)]
        prob = sb("prob", [P, 2 * G * N])
        probs = prob[:, :].rearrange("p (k g n) -> p k g n", k=2, g=G)
        qkf = prob[:, 0:3 * N].rearrange("p (c n) -> p c n", c=3)
        qkp = prob[:, 3 * N:3 * N + 9 * N // 2].bitcast(BF16).rearrange("p (c i n) -> p c i n", c=3, i=PARTS)
        oT = sb("oT", [P, 2, N])
        nmax = sb("nmax", [P, 2, 2 * NT])
        mres = sb("mres", [P, 2, 2 * NT])
        mpart = sb("mpart", [P, 2, PARTS, 2 * NT], BF16)
        mT = sb("mT", [PARTS * 2 * NT, 2, P], BF16)
        rec = sb("rec", [P, NT, G])
        big = sb("big", [P, CHH * N])
        hmid = big[:, :].rearrange("p (c n) -> p c n", n=N)
        wraw = big[0:ROWS, 0:WN]
        stats = sb("stats", [P, NT, 6])
        mv = sb("mv", [P, NT, 2])
        var = sb("var", [P, NT])
        rs = sb("rs", [P, NT])
        nw = sb("nw", [P, 2, NT])
        lg = sb("lg", [P, NT, E])
        cmp = sb("cmp", [P, 2, NT, E, E])
        rank = sb("rank", [P, NT, E])
        gmax = sb("gmax", [P, NT])
        gex = sb("gex", [P, NT, E])
        gsum = sb("gsum", [P, NT])
        cw = [sb(f"cw{b}", [P, NT, E]) for b in range(B)]
        y = sb("y", [P, NT, C])

        ld_x = [sem(f"ld_x{b}") for b in range(B)]
        ld_c = sem("ld_c")
        ld_ada = [sem(f"ld_ada{l}") for l in range(L)]
        ld_qkv = sem("ld_qkv")
        ld_raw = [sem("ld_raw0"), sem("ld_raw1")]
        ld_w = sem("ld_w")
        c_set = sem("c_set")
        c_ready = sem("c_ready")
        buf_ready = sem("buf_ready")
        s_full, s_free = sem("s_full"), sem("s_free")
        t_full, t_free = sem("t_full"), sem("t_free")
        silu_exp = sem("silu_exp")
        silu_done = sem("silu_done")
        w_ready = sem("w_ready")
        nat_ready = sem("nat_ready")
        qk_split = sem("qk_split")
        qk_out = [sem(f"qk_out{n}") for n in range(B * L)]
        qk_in = [sem(f"qk_in{n}") for n in range(B * L)]
        m_split = sem("m_split")
        m_out = sem("m_out")
        m_in = [sem(f"m_in{i}") for i in range(4)]
        p_used = sem("p_used")
        o_copied = sem("o_copied")
        x_ready = sem("x_ready")
        logit_ready = sem("logit_ready")
        gate_exp = sem("gate_exp")
        cw_ready = sem("cw_ready")
        dve_step = sem("dve_step")
        stored = sem("stored")

        block = ctx.enter_context(nc.Block())

        @block.sync
        def _(sp):
            def row(v):
                return v.rearrange("(a n) -> a n", a=1)

            names = (("L0_cond_w_adaln", "L0_cond_b_adaln"), ("L1_cond_w_ada", "L1_cond_b_ada"))
            sp.dma_start(x[:, 0], t["x"][0].rearrange("(t p) c -> p t c", p=P)).then_inc(ld_x[0], 16)
            for l, (w, bias) in enumerate(names):
                sp.dma_start(wada[l], t[w][0:P]).then_inc(ld_ada[l], 16)
                sp.dma_start(wadar[l][0:CR], t[w][P:C]).then_inc(ld_ada[l], 16)
                sp.dma_start(wadar[l][CR:CR + 1], row(t[bias])).then_inc(ld_ada[l], 16)
                if l == 0:
                    sp.dma_start(wqkv[0][:, :], t["L0_cond_w_qkv"][0:P]).then_inc(ld_qkv, 16)
                    sp.dma_start(x[:, 1], t["x"][1].rearrange("(t p) c -> p t c", p=P)).then_inc(ld_x[1], 16)

            def load_weights():
                sp.wait_ge(t_full, T_AT[WHERE[("ada", 1)] + 1])
                sp.dma_start(wproj[0][:, :], t["L0_cond_w_proj"][0:P]).then_inc(ld_w, 16)
                sp.dma_start(wgate[:, :], t["L0_cond_w_gate"][0:P]).then_inc(ld_w, 16)
                sp.dma_start(w1[:, :].rearrange("c (e h) -> c e h", e=E),
                             t["L0_cond_w1"][:, 0:P, :].rearrange("e c h -> c e h")).then_inc(ld_w, 16)
                w2f = t["L0_cond_w2"].rearrange("e h c -> (e h) c")
                sp.dma_start(w2[:, :].rearrange("p (k c) -> p k c", c=C),
                             w2f.rearrange("(k p) c -> p k c", p=P)).then_inc(ld_w, 16)
                sp.dma_start(wqkv[1][:, :], t["L1_cond_w_qkv"][0:P]).then_inc(ld_w, 16)
                sp.dma_start(wproj[1][:, :], t["L1_cond_w_proj"][0:P]).then_inc(ld_w, 16)
                sp.dma_start(wfc1[:, :], t["L1_cond_w_fc1"][0:P]).then_inc(ld_w, 16)
                full = HID // P
                sp.dma_start(wfc2[:, 0:full, :],
                             t["L1_cond_w_fc2"][0:full * P].rearrange("(k p) c -> p k c", p=P)).then_inc(ld_w, 16)
                sp.dma_start(wfc2[0:HID - full * P, full, :], t["L1_cond_w_fc2"][full * P:HID]).then_inc(ld_w, 16)
                sp.dma_start(b2bc[:, :, :], t["L0_cond_b2"].partition_broadcast(P)).then_inc(ld_w, 16)
                sp.dma_start(bfc2[:, :], t["L1_cond_b_fc2"].partition_broadcast(P)).then_inc(ld_w, 16)

            for i, stage in enumerate(SCHED):
                if stage[0] == "qkv":
                    _, l, b = stage
                    n = B * l + b
                    parts = qk_dram[n]
                    main = (HD - 1) * NH
                    for c, w, r, rows, lo in ((0, 0, 0, main, 0), (1, 1, 0, main, 0),
                                              (2, 0, 0, NH, main), (2, 1, NH, NH, main)):
                        sp.wait_ge(qk_split, 3 * n + c + 1)
                        sp.dma_start(parts[w, :, lo:lo + rows, :].rearrange("i r n -> r i n"),
                                     qkp[r:r + rows, c, :, :]).then_inc(qk_out[n], 16)
                    sp.wait_ge(qk_out[n], 4 * 16)
                    if n < B:
                        sp.wait_ge(buf_ready, 1)
                    else:
                        sp.wait_ge(t_full, scores_ended(n - B))
                    for i_ in range(PARTS):
                        r = HD * PARTS * i_
                        sp.dma_start(Ks[b][r:r + HD * PARTS, :, :],
                                     parts[1].rearrange("j (d h) n -> (j d) h n", h=NH)).then_inc(qk_in[n], 16)
                        for j in range(PARTS):
                            sp.dma_start(Qs[b][r + HD * j:r + HD * (j + 1), :, :],
                                         parts[0, i_].rearrange("(d h) n -> d h n", h=NH)).then_inc(qk_in[n], 16)
                    if n == 0:
                        load_weights()
                u = unit_of(stage)
                if u is not None and u % 2:
                    pair = (NH * stage[1] + u) // 2
                    n, h = stage[1] + u // NH, u % NH - 1
                    sp.wait_ge(t_free, T_AT[i + 1])
                    sp.dma_start(m_dram[pair].rearrange("i k q -> (i k) q"), mT[:, pair % 2, :]).then_inc(m_out, 16)
                    sp.wait_ge(m_out, 16 * (pair + 1))
                    if n < B:
                        sp.wait_ge(buf_ready, 1)
                    else:
                        sp.wait_ge(t_full, scores_ended(n - B))
                    sp.dma_start(Qs[n % B][MROW:SROWS, h:h + 2, :].rearrange("i h n -> i (h n)"),
                                 m_dram[pair].rearrange("i k q -> i (k q)")).then_inc(m_in[pair % 4], 16)

        @block.gpsimd
        def _(pool):
            nc.gpsimd.memset(ident[:, :], 0.0).then_inc(c_set, 1)
            nc.gpsimd.memset(identb[:, :], 0.0).then_inc(c_set, 1)
            nc.gpsimd.memset(mask1[:, :], -1.0).then_inc(c_set, 1)
            nc.gpsimd.memset(mask2[:, :], -1.0).then_inc(c_set, 1)
            nc.gpsimd.memset(before[:, :, :], 1.0).then_inc(c_set, 1)
            nc.gpsimd.memset(ones[:, :], 1.0).then_inc(c_ready, 1)
            nc.gpsimd.memset(wraw[:, WCOLS["gate"][0]:WCOLS["gate"][0] + E], 0.0).then_inc(c_set, 1)
            sources = {"qkv0": ("L0_cond_w_qkv", "L0_cond_b_qkv"), "proj0": ("L0_cond_w_proj", "L0_cond_b_proj"),
                       "gate": ("L0_cond_w_gate", None), "w1": ("L0_cond_w1", "L0_cond_b1"),
                       "qkv1": ("L1_cond_w_qkv", "L1_cond_b_qkv"), "proj1": ("L1_cond_w_proj", "L1_cond_b_proj"),
                       "fc1": ("L1_cond_w_fc1", "L1_cond_b_fc1")}

            def load_raw(name):
                done = ld_raw[name != "qkv0"]
                w, bias = sources[name]
                a, n = WCOLS[name]
                for rows in STACK.values():
                    for r, _ in rows:
                        if name == "w1":
                            pool.dma_start(wraw[r:r + CR, a:a + n].rearrange("c (e h) -> c e h", e=E),
                                           t[w][:, P:C, :].rearrange("e c h -> c e h")).then_inc(done, 16)
                        else:
                            pool.dma_start(wraw[r:r + CR, a:a + n], t[w][P:C, :]).then_inc(done, 16)
                for r in BIAS_ROWS:
                    if bias is not None:
                        src = t[bias].rearrange("e h -> (e h)") if name == "w1" else t[bias]
                        pool.dma_start(wraw[r:r + 1, a:a + n], src.rearrange("(o n) -> o n", o=1)).then_inc(done, 16)

            load_raw("qkv0")
            pool.wait_ge(c_set, 6)
            for m in (ident, identb):
                nc.gpsimd.affine_select(out=m[:, :], in_=m[:, :], compare_op=ALU.not_equal, fill=1.0, base=0,
                                        pattern=[[-1, P]], channel_multiplier=1).then_inc(c_ready, 1)
            for m, first in ((mask1, MASK1), (mask2, MASK2)):
                nc.gpsimd.affine_select(out=m[:, :], in_=m[:, :], compare_op=ALU.is_ge, fill=0.0, base=-first,
                                        pattern=[[0, 1]], channel_multiplier=1).then_inc(c_ready, 1)
            nc.gpsimd.affine_select(out=before[:, :, :], in_=before[:, :, :], compare_op=ALU.is_gt, fill=0.0, base=0,
                                    pattern=[[1, E], [-1, E]], channel_multiplier=0).then_inc(c_ready, 1)
            for name in sources:
                if name != "qkv0":
                    load_raw(name)

        @block.vector
        def _(dve):
            V = nc.vector
            step = [0]

            def link(ins):
                step[0] += 1
                ins.then_inc(dve_step, 1)
                dve.wait_ge(dve_step, step[0])

            def take(at):
                dve.wait_ge(s_full, at + 1)
                return S_BANKS[at % NS]

            turn_stages = [i for i, stage in enumerate(SCHED) if stage[0] == "turn"]
            prepared = [0]

            def natural_free():
                if prepared[0]:
                    dve.wait_ge(t_full, T_AT[turn_stages[prepared[0] - 1] + 1])
                prepared[0] += 1

            def split_stack(src):
                col = {part: [r for rows in STACK.values() for r, q in rows if q == part] for part in range(PARTS)}
                at = {part: [stN[:, :, r:r + CR] for r in rows] for part, rows in col.items()}
                yield V.tensor_copy(at[0][0], src)
                V.tensor_copy(at[0][1], at[0][0])
                V.tensor_copy(at[0][2], at[0][0])
                yield V.tensor_tensor(rest[:, :, :], src, at[0][0], ALU.subtract)
                yield V.tensor_copy(at[1][0], rest[:, :, :])
                yield V.tensor_copy(at[1][1], at[1][0])
                V.tensor_tensor(at[2][0], rest[:, :, :], at[1][0], ALU.subtract).then_inc(nat_ready, 1)

            def split_weights(a, n):
                raw, stk = wraw[:, a:a + n], wstk[:, a:a + n]
                link(V.tensor_copy(stk, raw))
                link(V.scalar_tensor_tensor(raw, stk, mask1[0:ROWS, 0:1], raw, ALU.mult, ALU.add))
                link(V.tensor_copy(stk, raw))
                link(V.scalar_tensor_tensor(stk, stk, mask2[0:ROWS, 0:1], raw, ALU.mult, ALU.add))

            def heads_innermost(l):
                a = WCOLS[f"qkv{l}"][0]
                for src, dst in ((wqkv[l][:, :], wqk[l][:, :]), (wstk[:, a:a + 3 * C], wqk_stk[l][:, :])):
                    for w in range(2):
                        V.tensor_copy(dst[:, w * P:(w + 1) * P].rearrange("p (d h) -> p d h", h=NH),
                                      src[:, w * C:(w + 1) * C].rearrange("p (h d) -> p d h", d=HD)[:, 0:HD - 1, :])
                    ins = V.tensor_copy(dst[:, 2 * P:2 * C], src[:, HD - 1:2 * C:HD])
                ins.then_inc(w_ready, 1)

            def layer_norm(l, b, shift, scale):
                for k in range(NT):
                    ins = V.bn_stats(stats[:, k, :], x[:, b, k, :])
                yield ins
                for k in range(NT):
                    ins = V.bn_aggr(mv[:, k, :], stats[:, k, :])
                yield ins
                yield V.tensor_scalar(var[:, :], mv[:, :, 1], EPS, None, ALU.add)
                bits = rs[:, :].bitcast(I32)
                yield V.tensor_single_scalar(bits, var[:, :].bitcast(I32), 1, ALU.arith_shift_right)
                yield V.tensor_scalar(bits, bits, -1.0, float(0x5F3759DF), ALU.mult, ALU.add)
                for _ in range(3):
                    yield V.tensor_tensor(nw[:, 0, :], rs[:, :], rs[:, :], ALU.mult)
                    yield V.scalar_tensor_tensor(nw[:, 1, :], nw[:, 0, :], -0.5, var[:, :], ALU.mult, ALU.mult)
                    yield V.scalar_tensor_tensor(rs[:, :], nw[:, 1, :], 1.5, rs[:, :], ALU.add, ALU.mult)
                natural_free()
                for k in range(NT):
                    ins = V.tensor_scalar(hN[:, k, :], x[:, b, k, :], mv[:, k, 0:1], rs[:, k:k + 1],
                                          ALU.subtract, ALU.mult)
                yield ins
                sc = mod[l][:, b, scale, :].unsqueeze(1).to_broadcast([P, NT, C])
                sh = mod[l][:, b, shift, :].unsqueeze(1).to_broadcast([P, NT, C])
                yield V.tensor_tensor(hN[:, :, :], hN[:, :, :], sc, ALU.mult)
                yield V.tensor_tensor(hN[:, :, :], hN[:, :, :], sh, ALU.add)
                yield from split_stack(hN[:, :, P:C])

            waiting = []

            def advance():
                if waiting:
                    gen, last = waiting[0]
                    if last is not None:
                        dve.wait_ge(dve_step, last)
                    ins = next(gen, None)
                    if ins is None:
                        waiting.pop()
                    else:
                        step[0] += 1
                        ins.then_inc(dve_step, 1)
                        waiting[0] = (gen, step[0])

            def run(gen):
                waiting.append((gen, None))
                while waiting:
                    advance()

            def gate_rows(l, b, gate, tiles):
                return mod[l][:, b, gate, :].unsqueeze(1).to_broadcast([P, tiles, C])

            for r in BIAS_ROWS:
                V.memset(stN[:, :, r:r + 1], 1.0)
            link(V.memset(siluBr[:, :, :], 1.0))

            def constant_rows():
                for b in range(B):
                    V.memset(Qs[b][64:96, :, :].bitcast(F32), 0.0)
                    V.memset(Ks[b][64:96, :, :].bitcast(F32), 0.0)
                    V.memset(Ks[b][96:SROWS, :, :], 1.0)
                    ins = V.memset(Va[b][:, :, :, :], 0.0)
                link(ins)
                for b in range(B):
                    ins = V.memset(Va[b][:, :, :, HD:HD + 1], 1.0)
                ins.then_inc(buf_ready, 1)

            for i, stage in enumerate(SCHED):
                kind, s_at = stage[0], S_AT[i]
                if kind == "ada":
                    l = stage[1]
                    if l == 0:
                        dve.wait_ge(silu_exp, 2)
                        V.tensor_scalar(ex[:, :], ex[:, :], 1.0, None, ALU.add)
                        link(V.tensor_scalar(exr[:, :], exr[:, :], 1.0, None, ALU.add))
                        V.reciprocal(ex[:, :], ex[:, :])
                        link(V.reciprocal(exr[:, :], exr[:, :]))
                        V.tensor_tensor(cT[:, :], cT[:, :], ex[:, :], ALU.mult)
                        link(V.tensor_tensor(cTr[:, :], cTr[:, :], exr[:, :], ALU.mult))
                        dve.wait_ge(c_ready, 6)
                        for b in range(B):
                            V.tensor_scalar(siluB[:, b, :], ones[:, :], cT[:, b:b + 1], None, ALU.mult)
                            ins = V.tensor_scalar(siluBr[0:CR, b, :], ones[0:CR, :], cTr[:, b:b + 1], None, ALU.mult)
                        ins.then_inc(silu_done, 1)
                        constant_rows()
                        dve.wait_ge(ld_raw[0], 16 * 9)
                        split_weights(*WCOLS["qkv0"])
                        dve.wait_ge(ld_qkv, 16)
                        heads_innermost(0)
                    dve.wait_ge(t_free, T_AT[i + 1])
                    for b in range(B):
                        for scale in (1, 4):
                            ins = V.tensor_scalar(mod[l][:, b, scale, :], mod[l][:, b, scale, :], 1.0, None, ALU.add)
                    link(ins)
                elif kind == "wsplit":
                    dve.wait_ge(ld_raw[1], 16 * (6 * 6 + 5 * 3))
                    a = WCOLS["proj0"][0]
                    split_weights(a, WN - a)
                    dve.wait_ge(ld_w, 16 * 11)
                    heads_innermost(1)
                elif kind == "ln":
                    _, l, which = stage
                    if l == 0 and which < B:
                        dve.wait_ge(ld_x[which], 16)
                    gen = layer_norm(l, which % B, 3 * (which // B), 3 * (which // B) + 1)
                    if which == 2:
                        waiting.append((gen, None))
                    else:
                        run(gen)
                elif kind == "turn":
                    while waiting:
                        advance()
                elif kind == "qkv":
                    _, l, b = stage
                    n = B * l + b
                    if n:
                        dve.wait_ge(qk_out[n - 1], 4 * 16)
                    chunks = ((0, P), (1, P), (2, 2 * NH))
                    for c, rows in chunks:
                        dve.wait_ge(t_free, T_AT[i] + c + 1)
                        link(V.tensor_copy(qkp[0:rows, c, 0, :], qkf[0:rows, c, :]))
                        link(V.tensor_tensor(qkf[0:rows, c, :], qkf[0:rows, c, :], qkp[0:rows, c, 0, :], ALU.subtract))
                        link(V.tensor_copy(qkp[0:rows, c, 1, :], qkf[0:rows, c, :]))
                        V.tensor_tensor(qkp[0:rows, c, 2, :], qkf[0:rows, c, :], qkp[0:rows, c, 1, :],
                                        ALU.subtract).then_inc(qk_split, 1)
                elif kind == "osplit":
                    _, l, b = stage
                    natural_free()
                    run(split_stack(oN[b][:, :, P:C]))
                elif kind == "proj":
                    _, l, b = stage
                    for k in range(NT // 2):
                        bank = take(s_at + k)
                        V.tensor_tensor(y[:, 2 * k:2 * k + 2, :], bank[:, 0:2 * C].rearrange("p (t c) -> p t c", t=2),
                                        gate_rows(l, b, 2, 2), ALU.mult).then_inc(s_free, 1)
                    dve.wait_ge(s_free, s_at + NT // 2)
                    link(V.tensor_tensor(x[:, b], x[:, b], y[:, :, :], ALU.add))
                elif kind == "gate":
                    b = stage[1]
                    bank = take(s_at)
                    V.tensor_copy(lg[:, :, :], bank[:, 0:NT * E].rearrange("p (t e) -> p t e", e=E)).then_inc(s_free, 1)
                    dve.wait_ge(s_free, s_at + 1)
                    me = lg[:, :, :].unsqueeze(3).to_broadcast([P, NT, E, E])
                    other = lg[:, :, :].unsqueeze(2).to_broadcast([P, NT, E, E])
                    V.tensor_tensor(cmp[:, 0], other, me, ALU.is_gt)
                    V.tensor_tensor(cmp[:, 1], other, me, ALU.is_equal)
                    link(V.tensor_reduce(gmax[:, :], lg[:, :, :], AX.X, ALU.max))
                    V.tensor_tensor(lg[:, :, :], lg[:, :, :], gmax[:, :].unsqueeze(2).to_broadcast([P, NT, E]),
                                    ALU.subtract).then_inc(logit_ready, 1)
                    early = before[:, :, :].unsqueeze(1).to_broadcast([P, NT, E, E])
                    link(V.tensor_tensor(cmp[:, 1], cmp[:, 1], early, ALU.mult))
                    link(V.tensor_tensor(cmp[:, 0], cmp[:, 0], cmp[:, 1], ALU.add))
                    link(V.tensor_reduce(rank[:, :, :], cmp[:, 0], AX.X, ALU.add))
                    dve.wait_ge(gate_exp, b + 1)
                    link(V.scalar_tensor_tensor(gex[:, :, :], rank[:, :, :], 2.0, gex[:, :, :], ALU.is_lt, ALU.mult))
                    link(V.tensor_reduce(gsum[:, :], gex[:, :, :], AX.X, ALU.add))
                    link(V.reciprocal(gsum[:, :], gsum[:, :]))
                    V.tensor_tensor(cw[b][:, :, :], gex[:, :, :], gsum[:, :].unsqueeze(2).to_broadcast([P, NT, E]),
                                    ALU.mult).then_inc(cw_ready, 1)
                elif kind == "fc2":
                    _, b, half = stage
                    if half == 0:
                        dve.wait_ge(cw_ready, b + 1)
                        dve.wait_ge(ld_w, 16 * 11)
                        for e in range(E):
                            for k in range(NT):
                                if e == 0:
                                    ins = V.tensor_scalar(y[:, k, :], b2bc[:, 0, :], cw[b][:, k, 0:1], None, ALU.mult)
                                else:
                                    ins = V.scalar_tensor_tensor(y[:, k, :], b2bc[:, e, :], cw[b][:, k, e:e + 1],
                                                                 y[:, k, :], ALU.mult, ALU.add)
                            link(ins)
                    for e in range(E2):
                        for k in range(NT):
                            at = s_at + NT * e + k
                            bank = take(at)
                            if k == 0 and e:
                                dve.wait_ge(s_free, at)
                            e_ = E2 * half + e
                            V.scalar_tensor_tensor(y[:, k, :], bank[:, 0:C], cw[b][:, k, e_:e_ + 1], y[:, k, :],
                                                   ALU.mult, ALU.add).then_inc(s_free, 1)
                    dve.wait_ge(s_free, S_AT[i + 1])
                    if half:
                        link(V.tensor_tensor(y[:, :, :], y[:, :, :], gate_rows(0, b, 5, NT), ALU.mult))
                        link(V.tensor_tensor(x[:, b], x[:, b], y[:, :, :], ALU.add))
                elif kind == "mlp2":
                    b = stage[1]
                    if b:
                        dve.wait_ge(x_ready, b)
                    for k in range(NT):
                        bank = take(s_at + k)
                        V.tensor_tensor(y[:, k, :], bank[:, 0:C], bfc2[:, :], ALU.add).then_inc(s_free, 1)
                    dve.wait_ge(s_free, S_AT[i + 1])
                    link(V.tensor_tensor(y[:, :, :], y[:, :, :], gate_rows(1, b, 5, NT), ALU.mult))
                    V.tensor_tensor(x[:, b], x[:, b], y[:, :, :], ALU.add).then_inc(x_ready, 1)

                u = unit_of(stage)
                if u is not None:
                    pair, odd = (NH * stage[1] + u) // 2, u % 2
                    half = pair % 2
                    if pair >= 2 and not odd:
                        dve.wait_ge(m_split, pair - 1)
                    for k in range(NT):
                        bank = take(s_at + k)
                        V.tensor_reduce(nmax[:, half, odd * NT + k:odd * NT + k + 1], bank[:, :], AX.X, ALU.max,
                                        negate=True).then_inc(s_free, 1)
                        advance()
                    if odd:
                        if pair >= 2:
                            dve.wait_ge(t_full, pair_turned(pair - 2))
                        dve.wait_ge(s_free, s_at + NT)
                        link(V.tensor_copy(mpart[:, half, 0, :], nmax[:, half, :]))
                        link(V.tensor_tensor(mres[:, half, :], nmax[:, half, :], mpart[:, half, 0, :], ALU.subtract))
                        link(V.tensor_copy(mpart[:, half, 1, :], mres[:, half, :]))
                        V.tensor_tensor(mpart[:, half, 2, :], mres[:, half, :], mpart[:, half, 1, :],
                                        ALU.subtract).then_inc(m_split, 1)
                g, k = finishes(stage)
                if k == 2:
                    b, hg = g // HG, g % HG
                    at = S_AT[i + 1] - 1
                    o = take(at)[:, :].rearrange("p (t g w) -> p t g w", t=NT, g=G)
                    link(V.reciprocal(rec[:, :, :], o[:, :, :, HD]))
                    dst = oN[b][:, :, hg * G * HD:(hg + 1) * G * HD].rearrange("p t (g d) -> p t g d", d=HD)
                    V.tensor_tensor(dst, o[:, :, :, 0:HD], rec[:, :, :].unsqueeze(3).to_broadcast([P, NT, G, HD]),
                                    ALU.mult).then_inc(s_free, 1)
                    dve.wait_ge(s_free, at + 1)

        @block.scalar
        def _(act):
            A = nc.scalar
            last_use = {}

            def take(at):
                act.wait_ge(t_full, at + 1)
                return T_BANKS[at % NTB]

            act.dma_start(cT[:, :], t["cond_1152"][:, 0:P].rearrange("b c -> c b"),
                          allow_slow_non_contiguous=True).then_inc(ld_c, 16)
            act.dma_start(cTr[:, :], t["cond_1152"][:, P:C].rearrange("b c -> c b"),
                          allow_slow_non_contiguous=True).then_inc(ld_c, 16)

            for i, stage in enumerate(SCHED):
                kind, t_at = stage[0], T_AT[i]
                if kind == "ada":
                    l = stage[1]
                    if l == 0:
                        act.wait_ge(ld_c, 32)
                        A.activation(ex[:, :], cT[:, :], ACT.Exp, scale=-1.0).then_inc(silu_exp, 1)
                        A.activation(exr[:, :], cTr[:, :], ACT.Exp, scale=-1.0).then_inc(silu_exp, 1)
                    for b in range(B):
                        for half in range(2):
                            bank = take(t_at + 2 * b + half)
                            A.activation(mod[l][:, b, 3 * half:3 * half + 3, :].rearrange("p s c -> p (s c)"),
                                         bank[:, 0:3 * C], ACT.Copy).then_inc(t_free, 1)
                elif kind == "turn":
                    _, l, b, buf = stage
                    key = buf if buf == "a" else (buf, b)
                    if key in last_use:
                        j = last_use[key]
                        if SCHED[j][0] == "proj":
                            act.wait_ge(s_full, S_AT[j + 1])
                        else:
                            act.wait_ge(t_full, T_AT[j + 1])
                    last_use[key] = tile_used(i)
                    bank = take(t_at)
                    A.activation(hT[buf][b][:, :], bank[:, :], ACT.Copy).then_inc(t_free, 1)
                    bank = take(t_at + 1)
                    A.activation(hS[buf][b][:, :], bank[0:ROWS, 0:N // 2].bitcast(BF16), ACT.Copy).then_inc(t_free, 1)
                elif kind == "qkv":
                    _, l, b = stage
                    n = B * l + b
                    if n:
                        act.wait_ge(qk_split, 3 * n)
                    if n >= B and b == 0:
                        act.wait_ge(p_used, NT * B * HG)
                    for c, rows in ((0, P), (1, P), (2, 2 * NH)):
                        bank = take(t_at + c)
                        A.activation(qkf[0:rows, c, :], bank[0:rows, :], ACT.Copy).then_inc(t_free, 1)
                    if n < B:
                        act.wait_ge(buf_ready, 1)
                    else:
                        act.wait_ge(p_used, NT * HG * (n - 1))
                    for k in range(NT // 2):
                        bank = take(t_at + 3 + k)
                        A.activation(Va[b][:, 2 * k:2 * k + 2, :, 0:HD],
                                     bank[:, 0:2 * C].rearrange("p (t h d) -> p t h d", t=2, d=HD),
                                     ACT.Copy).then_inc(t_free, 1)
                elif kind == "gate":
                    b = stage[1]
                    act.wait_ge(logit_ready, b + 1)
                    if b:
                        act.wait_ge(cw_ready, b)
                    A.activation(gex[:, :, :], lg[:, :, :], ACT.Exp).then_inc(gate_exp, 1)
                elif kind in ("fc1", "mlp1"):
                    prev = [j for j in range(i) if SCHED[j][0] in ("fc2", "mlp2")]
                    if prev:
                        act.wait_ge(s_full, S_AT[prev[-1] + 1])
                    if kind == "fc1" and stage[1:] == (0, 0):
                        act.wait_ge(w_ready, 2)
                    for c in range(CHH if kind == "fc1" else CH1):
                        rows = P if kind == "fc1" else min(P, HID - c * P)
                        bank = take(t_at + c)
                        A.activation(hmid[0:rows, c, :], bank[0:rows, :], ACT.Gelu_apprx_tanh).then_inc(t_free, 1)
                if kind == "slot":
                    _, n0, g, k = stage
                    done = NT * (HG * n0 + g) + k
                    if g == 0 and k == 0:
                        act.wait_ge(qk_out[n0 + 1], 4 * 16)
                    for j in range(G):
                        bank = take(t_at + j)
                        if done >= 2 and j == 0:
                            act.wait_ge(p_used, done - 1)
                        A.activation(probs[:, k % 2, j, :], bank[:, :], ACT.Exp, scale=SCALE).then_inc(t_free, 1)
                u = unit_of(stage)
                if u is not None and u % 2:
                    pair = (NH * stage[1] + u) // 2
                    if pair >= 2:
                        act.wait_ge(m_out, 16 * (pair - 1))
                    bank = take(T_AT[i + 1] - 1)
                    A.activation(mT[:, pair % 2, :], bank[0:PARTS * 2 * NT, 0:P // 2].bitcast(BF16), ACT.Copy)\
                        .then_inc(t_free, 1)
                g, k = finishes(stage)
                if k == 1:
                    gn = HG * stage[1] + g
                    act.wait_ge(p_used, NT * (gn + 1))
                    if gn >= 2:
                        act.wait_ge(s_full, turned_back(gn - 2))
                    A.activation(oT[:, gn % 2, :], O_BANKS[gn % 2][:, :], ACT.Copy).then_inc(o_copied, 1)
            for b in range(B):
                act.wait_ge(x_ready, b + 1)
                act.dma_start(out[b].rearrange("(t p) c -> p t c", p=P), x[:, b]).then_inc(stored, 16)
            act.wait_ge(stored, 16 * B)

        @block.tensor
        def _(pe):
            M = nc.tensor
            turns = [0]

            def fill_s(at):
                if at >= NS:
                    pe.wait_ge(s_free, at - NS + 1)
                return S_BANKS[at % NS]

            def fill_t(at):
                if at >= NTB:
                    pe.wait_ge(t_free, at - NTB + 1)
                return T_BANKS[at % NTB]

            def stacked(name, lo, hi):
                a, _ = WCOLS[name]
                return wstk[:, a + lo:a + hi]

            def second(n0, g, k):
                gn = HG * n0 + g
                b, h0 = g // HG, G * (g % HG)
                if k == 0 and gn >= 2:
                    pe.wait_ge(o_copied, gn - 1)
                pe.wait_ge(t_free, T_AT[WHERE[("slot", n0, g, k)]] + G)
                for j in range(G):
                    ins = M.matmul(O_BANKS[gn % 2][OW * j:OW * (j + 1), :], Va[b][:, k, h0 + j, :],
                                   probs[:, k % 2, j, :], start=(k == 0), stop=(k == NT - 1), skip_group_check=True)
                ins.then_inc(p_used, 1)

            for i, stage in enumerate(SCHED):
                kind, s_at, t_at = stage[0], S_AT[i], T_AT[i]
                if kind == "ada":
                    l = stage[1]
                    pe.wait_ge(silu_done, 1)
                    pe.wait_ge(ld_ada[l], 48)
                    for b in range(B):
                        for half in range(2):
                            bank = fill_t(t_at + 2 * b + half)
                            cols = slice(3 * C * half, 3 * C * (half + 1))
                            M.matmul(bank[:, 0:3 * C], siluB[:, b, :], wada[l][:, cols], start=True, stop=False)
                            M.matmul(bank[:, 0:3 * C], siluBr[:, b, :], wadar[l][:, cols], start=False, stop=True)\
                                .then_inc(t_full, 1)
                elif kind == "turn":
                    _, l, b, buf = stage
                    turns[0] += 1
                    if turns[0] == 1:
                        pe.wait_ge(c_ready, 6)
                    pe.wait_ge(nat_ready, turns[0])
                    src = oN[b] if SCHED[i - 1][0] == "osplit" else hN
                    bank = fill_t(t_at)
                    for k in range(NT):
                        ins = M.transpose(bank[:, k * P:(k + 1) * P], src[:, k, 0:P], ident[:, :])
                    ins.then_inc(t_full, 1)
                    view = fill_t(t_at + 1)[0:ROWS, 0:N // 2].bitcast(BF16)
                    for k in range(NT):
                        ins = M.transpose(view[:, k * P:(k + 1) * P], stN[:, k, 0:ROWS], identb[:, :])
                    ins.then_inc(t_full, 1)
                elif kind == "qkv":
                    _, l, b = stage
                    h, s = hT["a"][b], hS["a"][b]
                    pe.wait_ge(t_free, t_at)
                    pe.wait_ge(w_ready, 1 + l)
                    pe.wait_ge(*((ld_qkv, 16) if l == 0 else (ld_w, 16 * 11)))
                    name = f"qkv{l}"

                    for c, lo, cols in ((0, 0, P), (1, P, P), (2, 2 * P, 2 * NH)):
                        bank = fill_t(t_at + c)
                        M.matmul(bank[0:cols, :], wqk[l][:, lo:lo + cols], h[:, :], start=True, stop=False)
                        M.matmul(bank[0:cols, :], wqk_stk[l][:, lo:lo + cols], s[:, :],
                                 start=False, stop=True).then_inc(t_full, 1)
                    for k2 in range(NT // 2):
                        bank = fill_t(t_at + 3 + k2)
                        for k in range(2):
                            at = slice((2 * k2 + k) * P, (2 * k2 + k + 1) * P)
                            M.matmul(bank[:, k * C:(k + 1) * C], h[:, at], wqkv[l][:, 2 * C:3 * C],
                                     start=True, stop=False)
                            ins = M.matmul(bank[:, k * C:(k + 1) * C], s[:, at], stacked(name, 2 * C, 3 * C),
                                           start=False, stop=True)
                        ins.then_inc(t_full, 1)
                elif kind == "proj":
                    _, l, b = stage
                    h, s = hT["a"][b], hS["a"][b]
                    pe.wait_ge(t_free, t_at)
                    pe.wait_ge(w_ready, 2)
                    pe.wait_ge(ld_w, 16 * 11)
                    for k2 in range(NT // 2):
                        bank = fill_s(s_at + k2)
                        for k in range(2):
                            at = slice((2 * k2 + k) * P, (2 * k2 + k + 1) * P)
                            M.matmul(bank[:, k * C:(k + 1) * C], h[:, at], wproj[l][:, :], start=True, stop=False)
                            ins = M.matmul(bank[:, k * C:(k + 1) * C], s[:, at], stacked(f"proj{l}", 0, C),
                                           start=False, stop=True)
                        ins.then_inc(s_full, 1)
                elif kind == "gate":
                    b = stage[1]
                    h, s = hT["b"][b], hS["b"][b]
                    pe.wait_ge(t_free, t_at)
                    bank = fill_s(s_at)
                    for k in range(NT):
                        at = slice(k * P, (k + 1) * P)
                        M.matmul(bank[:, k * E:(k + 1) * E], h[:, at], wgate[:, :], start=True, stop=False)
                        ins = M.matmul(bank[:, k * E:(k + 1) * E], s[:, at], stacked("gate", 0, E),
                                       start=False, stop=True)
                    ins.then_inc(s_full, 1)
                elif kind in ("fc1", "mlp1"):
                    b = stage[1]
                    h, s = hT["b"][b], hS["b"][b]
                    name, w, base, n = ("w1", w1, CHH * stage[2], CHH) if kind == "fc1" else ("fc1", wfc1, 0, CH1)
                    pe.wait_ge(t_free, T_AT[WHERE[("turn", 0 if kind == "fc1" else 1, b, "b")] + 1])
                    for c in range(n):
                        rows = P if kind == "fc1" else min(P, HID - c * P)
                        lo = (base + c) * P
                        bank = fill_t(t_at + c)
                        M.matmul(bank[0:rows, :], w[:, lo:lo + rows], h[:, :], start=True, stop=False)
                        M.matmul(bank[0:rows, :], stacked(name, lo, lo + rows), s[:, :], start=False, stop=True)\
                            .then_inc(t_full, 1)
                elif kind in ("fc2", "mlp2"):
                    b = stage[1]
                    first = ("fc1",) + stage[1:] if kind == "fc2" else ("mlp1", b)
                    pe.wait_ge(t_free, T_AT[WHERE[first] + 1])
                    for e in range(E2 if kind == "fc2" else 1):
                        for k in range(NT):
                            bank = fill_s(s_at + NT * e + k)
                            if kind == "fc2":
                                parts = hidden_parts(e)
                            else:
                                parts = [(c, 0, min(P, HID - c * P)) for c in range(CH1)]
                            for c, lo, hi in parts:
                                if kind == "fc2":
                                    chunk = CHH * stage[2] + c
                                    w = w2[lo:hi, chunk * C:(chunk + 1) * C]
                                else:
                                    w = wfc2[lo:hi, c, :]
                                ins = M.matmul(bank[:, 0:C], hmid[lo:hi, c, k * P:(k + 1) * P], w,
                                               start=(c == parts[0][0]), stop=(c == parts[-1][0]))
                            ins.then_inc(s_full, 1)

                u = unit_of(stage)
                for k4 in range(NT):
                    if u is not None:
                        n, h_ = stage[1] + u // NH, u % NH
                        b = n % B
                        if k4 == 0 and h_ == 0:
                            pe.wait_ge(qk_in[n], 16 * 12)
                        bank = fill_s(s_at + k4)
                        M.matmul(bank[:, :], Qs[b][0:MROW, h_, k4 * P:(k4 + 1) * P], Ks[b][0:MROW, h_, :],
                                 start=True, stop=True).then_inc(s_full, 1)
                    if kind == "slot":
                        _, n0, g, k = stage
                        b, h0 = g // HG, G * (g % HG)
                        if k == 0 and k4 % 2 == 0:
                            pair = (NH * n0 + G * g + k4) // 2
                            pe.wait_ge(m_in[pair % 4], 16 * (pair // 4 + 1))
                        bank = fill_t(t_at + k4)
                        M.matmul(bank[:, :], Ks[b][0:SROWS, h0 + k4, k * P:(k + 1) * P], Qs[b][0:SROWS, h0 + k4, :],
                                 start=True, stop=True).then_inc(t_full, 1)
                if kind == "slot" and (g or k):
                    second(n0, *((g, k - 1) if k else (g - 1, NT - 1)))
                if kind == "tail" and stage[2] == 0:
                    second(stage[1], B * HG - 1, NT - 1)
                if u is not None and u % 2:
                    pair = (NH * stage[1] + u) // 2
                    pe.wait_ge(m_split, pair + 1)
                    view = fill_t(T_AT[i + 1] - 1)[0:PARTS * 2 * NT, 0:P // 2].bitcast(BF16)
                    M.transpose(view, mpart[:, pair % 2, :, :].rearrange("p i k -> p (i k)"), identb[:, :])\
                        .then_inc(t_full, 1)
                g, k = finishes(stage)
                if k == 2:
                    gn = HG * stage[1] + g
                    pe.wait_ge(o_copied, gn + 1)
                    bank = fill_s(S_AT[i + 1] - 1)
                    for q in range(NT):
                        ins = M.transpose(bank[:, q * P:(q + 1) * P], oT[:, gn % 2, q * P:(q + 1) * P], ident[:, :])
                    ins.then_inc(s_full, 1)


def kernel(**inputs):
    import numpy as _np
    import concourse.bacc as _bacc
    from concourse import mybir as _mybir
    from concourse.bass_utils import run_bass_kernel_spmd as _run

    nc = _bacc.Bacc("TRN2", target_bir_lowering=False, num_devices=1)
    arrays, args = {}, {}
    for name, value in inputs.items():
        a = _np.ascontiguousarray(value)
        arrays[f"in_{name}_dram"] = a
        args[name] = nc.dram_tensor(f"in_{name}_dram", a.shape, _mybir.dt.from_np(a.dtype),
                                    kind="ExternalInput").ap()
    out = nc.dram_tensor("out_0_dram", (B, N, C), F32, kind="ExternalOutput").ap()
    build(nc, args, out)
    r = _run(nc, [arrays], core_ids=[0])
    return r.results[0]["out_0_dram"]
```

```python
from contextlib import ExitStack

import concourse.bass as bass
from concourse import mybir

F32 = mybir.dt.float32
BF16 = mybir.dt.bfloat16
I32 = mybir.dt.int32
ALU = mybir.AluOpType
ACT = mybir.ActivationFunctionType
AX = mybir.AxisListType

P = 128
B, N, C = 2, 512, 144
NT = N // P
NH, HD = 16, 9
CR = C - P
E, HID = 4, 4 * C
CH = E * HID // P
E2 = E // 2
CHH = CH // 2
CH1 = -(-HID // P)
L = 2
EPS = 1e-6
SCALE = HD ** -0.5
PARTS = 3
PAIRS = PARTS * PARTS * HD
MROW = 96
MPARTS = 2
SROWS = MROW + MPARTS
G = 4
HG = NH // G
UNIT_LEAD = 6
OW = 32

STACK = {0: ((0, 2), (16, 1), (32, 0)), 1: ((49, 1), (65, 0)), 2: ((82, 0),)}
BIAS_ROWS = (48, 81, 98)
ROWS = 99
MASK1, MASK2 = 49, 82

WCOLS = {}
_at = 0
for _name, _n in (("qkv0", 3 * C), ("proj0", C), ("gate", E), ("w1", E * HID),
                  ("qkv1", 3 * C), ("proj1", C), ("fc1", HID)):
    WCOLS[_name] = (_at, _n)
    _at += _n
WN = _at


def schedule():
    s = [("ada", 0, 0), ("lnstat",), ("ln", 0, 0), ("ada", 0, 1), ("ada", 0, 2), ("turn", 0, 0, "a"), ("ln", 0, 1),
         ("qkv", 0, 0), ("turn", 0, 1, "a"), ("qkv", 0, 1), ("ada", 1, 0), ("ada", 1, 1), ("ada", 1, 2)]
    s += [("max", 0, u) for u in range(UNIT_LEAD)]
    for l in range(L):
        n0 = B * l
        after = {(4, 3): [("osplit", l, 0)], (5, 0): [("turn", l, 0, "a")], (5, 1): [("proj", l, 0), ("ln", l, 2)],
                 (7, 1): [("turn", l, 0, "b")]}
        if l == 0:
            after[7, 2] = [("gate", 0)]
        else:
            after[0, 2] = [("turn", l, 1, "a")]
            after[0, 3] = [("qkv", l, 1)]
        for g in range(B * HG):
            for k in range(NT):
                s += [("slot", n0, g, k)] + after.get((g, k), [])
        s += [("tail", n0, 0)]
        if l == 0:
            s += [("fc1", 0, 0, 0, 5), ("tail", n0, 1), ("tail", n0, 2), ("osplit", l, 1), ("fc1", 0, 0, 5, CHH),
                  ("turn", l, 1, "a"), ("fc2", 0, 0, 0), ("proj", l, 1), ("ln", l, 3), ("fc2", 0, 0, 1),
                  ("fc1", 0, 1, 0, CHH), ("turn", l, 1, "b"), ("fc2", 0, 1, 0), ("gate", 1), ("fc2", 0, 1, 1),
                  ("ln", 1, 0), ("fc1", 1, 0, 0, CHH), ("turn", 1, 0, "a"), ("fc2", 1, 0, 0), ("qkv", 1, 0),
                  ("fc2", 1, 0, 1)]
            s += [("fc1", 1, 1, 0, 4), ("max", B, 0), ("fc1", 1, 1, 4, 6), ("max", B, 1), ("fc1", 1, 1, 6, 8),
                  ("max", B, 2), ("fc1", 1, 1, 8, CHH), ("max", B, 3), ("fc2", 1, 1, 0), ("max", B, 4), ("fc2", 1, 1, 1),
                  ("ln", 1, 1), ("max", B, 5)]
            s += [("max", B, u) for u in range(6, UNIT_LEAD)]
        else:
            s += [("mlp1", 0), ("tail", n0, 1), ("tail", n0, 2), ("osplit", l, 1), ("turn", l, 1, "a"),
                  ("proj", l, 1), ("ln", l, 3), ("mlp2", 0), ("turn", l, 1, "b"), ("mlp1", 1), ("mlp2", 1)]
    return s


SCHED = schedule()


LATE0, LATE1 = 10, 6


PIECES = (((0, G), (G, NH)), tuple((h, h + G) for h in range(0, NH, G)))
PIECES_AT = (((0, 1), (0, 3), (1, 1), (1, 3)), ((1, 3), (2, 0), (2, 2), (3, 0)))


def pieces_after(stage):
    if stage[0] == "qkv" and stage[2] == 0:
        return [(B * stage[1], piece) for piece in range(len(PIECES[0]))]
    if stage[0] == "slot" and stage[2:] in PIECES_AT[stage[1] // B]:
        return [(stage[1] + 1, PIECES_AT[stage[1] // B].index(stage[2:]))]
    return []


def unit_of(stage):
    u = stage[2] if stage[0] == "max" else NT * stage[2] + stage[3] + UNIT_LEAD if stage[0] == "slot" else None
    return u if u is not None and u < B * NH else None


def turns_pair(stage):
    if stage[0] not in ("max", "slot"):
        return None
    u = stage[2] if stage[0] == "max" else NT * stage[2] + stage[3] + UNIT_LEAD
    return (NH * stage[1] + u) // 2 - 1 if u % 2 == 0 and 2 <= u <= B * NH else None


def finishes(stage):
    if stage[0] == "slot" and stage[2]:
        return stage[2] - 1, stage[3]
    if stage[0] == "tail":
        return B * HG - 1, stage[2]
    return None, None


def banks_used(stage):
    kind, s, t = stage[0], 0, 0
    if kind == "ada":
        t = B if stage[1:] == (0, 0) else 1
    elif kind == "turn":
        t = 2
    elif kind == "qkv":
        t = 3 + NT // 2
    elif kind == "proj":
        s = NT // 2
    elif kind == "gate":
        s = 1
    elif kind == "fc1":
        t = stage[4] - stage[3]
    elif kind == "fc2":
        s = NT
    elif kind == "mlp1":
        t = CH1
    elif kind == "mlp2":
        s = NT
    if kind == "slot":
        t += G
    u = unit_of(stage)
    if u is not None:
        s += NT
    if turns_pair(stage) is not None:
        t += 1
    if finishes(stage)[1] == 2:
        s += 1
    return s, t


S_AT, T_AT = [0], [0]
for _stage in SCHED:
    _s, _t = banks_used(_stage)
    S_AT.append(S_AT[-1] + _s)
    T_AT.append(T_AT[-1] + _t)
WHERE = {}
for _i, _stage in enumerate(SCHED):
    WHERE[_stage] = _i


PAIR_STAGE = [i for i, stage in enumerate(SCHED) if turns_pair(stage) is not None]


def pair_turned(pair):
    return T_AT[PAIR_STAGE[pair] + 1]


def tile_used(i):
    _, l, b, buf = SCHED[i]
    if buf == "b":
        return max(j for j, s in enumerate(SCHED)
                   if j > i and (s[:2] == ("fc1", b) if l == 0 else s == ("mlp1", b)))
    return min(j for j, s in enumerate(SCHED) if j > i and s[0] in ("qkv", "proj"))


BACK_STAGE = [i for i, stage in enumerate(SCHED) if finishes(stage)[1] == 2]


def turned_back(gn):
    return S_AT[BACK_STAGE[gn] + 1]


def scores_ended(n):
    n0, b = n - n % B, n % B
    return T_AT[WHERE[("slot", n0, HG * (b + 1) - 1, NT - 1)]] + G


def hidden_parts(e):
    lo, parts = (e % E2) * HID, []
    while lo < (e % E2 + 1) * HID:
        hi = min((lo // P + 1) * P, (e % E2 + 1) * HID)
        parts.append((lo // P, lo % P, lo % P + hi - lo))
        lo = hi
    return parts


def build(nc, t, out):
    ctx = ExitStack()
    with ctx:
        def sb(name, shape, dt=F32):
            return ctx.enter_context(nc.sbuf_tensor(name, shape, dt))

        def sem(name):
            return ctx.enter_context(nc.semaphore(name))

        banks = [ctx.enter_context(nc.psum_tensor(f"bank{i}", [P, 512], F32)) for i in range(8)]
        S_BANKS, T_BANKS, O_BANKS = banks[0:3], banks[3:6], banks[6:8]
        NS, NTB = len(S_BANKS), len(T_BANKS)

        qk_dram = nc.dram_tensor("qk_parts", (B * L, 2, PARTS, HD * NH, N), BF16, kind="Internal").ap()
        mod_dram = nc.dram_tensor("modulation", (L, 3, B, 2, C), F32, kind="Internal").ap()

        ident = sb("ident", [P, P])
        identb = sb("identb", [P, P], BF16)
        ones = sb("ones", [P, P])
        mask1 = sb("mask1", [P, 1])
        mask2 = sb("mask2", [P, 1])
        before = sb("before", [P, E, E])
        wqkv = [sb(f"wqkv{l}", [P, 3 * C]) for l in range(L)]
        wqk = [sb(f"wqk{l}", [P, 2 * C]) for l in range(L)]
        wqk_stk = [sb(f"wqk_stk{l}", [ROWS, 2 * C], BF16) for l in range(L)]
        wproj = [sb(f"wproj{l}", [P, C]) for l in range(L)]
        wgate = sb("wgate", [P, E])
        w1 = sb("w1", [P, E * HID])
        w2 = sb("w2", [P, CH * C])
        wfc1 = sb("wfc1", [P, HID])
        wfc2 = sb("wfc2", [P, CH1, C])
        wstk = sb("wstk", [ROWS, WN], BF16)
        b2bc = sb("b2bc", [P, E, C])
        bfc2 = sb("bfc2", [P, C])
        wada = [w1[:, l * 6 * C:(l + 1) * 6 * C] for l in range(L)]
        wadar = [w2[0:CR + 1, l * 6 * C:(l + 1) * 6 * C] for l in range(L)]
        cT = sb("cT", [P, B])
        cTr = sb("cTr", [CR, B])
        ex = sb("ex", [P, B])
        exr = sb("exr", [CR, B])
        siluB = sb("siluB", [P, B, P])
        siluBr = sb("siluBr", [CR + 1, B, P])
        mod = [sb(f"mod{l}", [P, B, 6, C]) for l in range(L)]
        x = sb("x", [P, B, NT, C])
        hN = sb("hN", [P, NT, C])
        stN = sb("stN", [P, NT, 100], BF16)
        rest = sb("rest", [P, NT, CR])
        oN = [sb(f"oN{b}", [P, NT, C]) for b in range(B)]
        hT = {"a": [sb("hTa", [P, N])] * B, "b": [sb(f"hTb{b}", [P, N]) for b in range(B)]}
        hS = {"a": [sb("hSa", [ROWS, N], BF16)] * B, "b": [sb(f"hSb{b}", [ROWS, N], BF16) for b in range(B)]}
        Qs = [sb(f"Qs{b}", [P, NH, N], BF16) for b in range(B)]
        Ks = [sb(f"Ks{b}", [P, NH, N], BF16) for b in range(B)]
        Va = [sb(f"Va{b}", [P, NT, NH, OW]) for b in range(B)]
        prob = sb("prob", [P, 2 * G * N])
        probs = prob[:, :].rearrange("p (k g n) -> p k g n", k=2, g=G)
        oT = sb("oT", [P, 2, N])
        nmax = sb("nmax", [P, 2, 2 * NT])
        mpart = sb("mpart", [P, 2, MPARTS, 2 * NT], BF16)
        mT = sb("mT", [MPARTS * 2 * NT, 2, P], BF16)
        rec = sb("rec", [P, NT, G])
        big = sb("big", [P, CHH * N])
        hmid = big[:, :].rearrange("p (c n) -> p c n", n=N)
        wraw = big[0:ROWS, 0:WN]
        qkf, qkp = [], []
        for place in (prob, prob, prob, big):
            qkf.append(place[:, 0:3 * N].rearrange("p (c n) -> p c n", c=3))
            qkp.append(place[:, 3 * N:3 * N + 9 * N // 2].bitcast(BF16)
                       .rearrange("p (c i n) -> p c i n", c=3, i=PARTS))
        stats = sb("stats", [P, B, NT, 6])
        mv = sb("mv", [P, B, NT, 2])
        var = sb("var", [P, B, NT])
        rs = sb("rs", [P, B, NT])
        nw = sb("nw", [P, B, 2, NT])
        lg = sb("lg", [P, NT, E])
        cmp = sb("cmp", [P, 2, NT, E, E])
        rank = sb("rank", [P, NT, E])
        gmax = sb("gmax", [P, NT])
        gex = sb("gex", [P, NT, E])
        gsum = sb("gsum", [P, NT])
        cw = [sb(f"cw{b}", [P, NT, E]) for b in range(B)]
        y = sb("y", [P, NT, C])
        attn = sb("attn", [P, NT, C])
        mod_row = {(l, part): place[0:B, 2 * half:2 * half + 2, :]
                   for l, part, place, half in ((0, 1, y, 0), (0, 2, y, 1), (1, 0, attn, 0), (1, 1, attn, 1),
                                                (1, 2, oN[1], 0))}

        ld_x = [sem(f"ld_x{b}") for b in range(B)]
        ld_c = sem("ld_c")
        ld_ada = [sem(f"ld_ada{l}") for l in range(L)]
        ld_qkv = sem("ld_qkv")
        ld_raw = [sem("ld_raw0"), sem("ld_raw1")]
        ld_w = [sem(f"ld_w{l}") for l in range(L)]
        c_ready = sem("c_ready")
        buf_ready = sem("buf_ready")
        v_ready = [sem(f"v_ready{b}") for b in range(B)]
        s_full, s_free = sem("s_full"), sem("s_free")
        t_full, t_free = sem("t_full"), sem("t_free")
        silu_exp = sem("silu_exp")
        silu_done = sem("silu_done")
        mod_out = sem("mod_out")
        mod_in = [[sem(f"mod_in{l}{part}") for part in range(3)] for l in range(L)]
        w_split = sem("w_split")
        w_ready = sem("w_ready")
        pool_step = sem("pool_step")
        nat_ready = sem("nat_ready")
        qk_split = sem("qk_split")
        qk_out = [sem(f"qk_out{n}") for n in range(B * L)]
        qk_in = [[sem(f"qk_in{n}_{i}") for i in range(len(PIECES[n % B]))] for n in range(B * L)]
        m_first = sem("m_first")
        m_split = sem("m_split")
        m_in = [sem(f"m_in{i}") for i in range(4)]
        p_used = sem("p_used")
        o_copied = sem("o_copied")
        x_ready = sem("x_ready")
        logit_ready = sem("logit_ready")
        gate_exp = sem("gate_exp")
        cw_ready = sem("cw_ready")
        dve_step = sem("dve_step")
        stored = sem("stored")

        block = ctx.enter_context(nc.Block())

        @block.sync
        def _(sp):
            def row(v):
                return v.rearrange("(a n) -> a n", a=1)

            names = (("L0_cond_w_adaln", "L0_cond_b_adaln"), ("L1_cond_w_ada", "L1_cond_b_ada"))
            for b in range(B):
                sp.dma_start(x[:, b], t["x"][b].rearrange("(t p) c -> p t c", p=P)).then_inc(ld_x[b], 16)
            for l, (w, bias) in enumerate(names):
                sp.dma_start(wada[l], t[w][0:P]).then_inc(ld_ada[l], 16)
                sp.dma_start(wadar[l][0:CR], t[w][P:C]).then_inc(ld_ada[l], 16)
                sp.dma_start(wadar[l][CR:CR + 1], row(t[bias])).then_inc(ld_ada[l], 16)
                if l == 0:
                    sp.dma_start(wqkv[0][:, :], t["L0_cond_w_qkv"][0:P]).then_inc(ld_qkv, 16)

            w2f = t["L0_cond_w2"].rearrange("e h c -> (e h) c").rearrange("(k p) c -> p k c", p=P)
            full = HID // P
            late = [(0, wproj[0][:, :], t["L0_cond_w_proj"][0:P]), (0, wgate[:, :], t["L0_cond_w_gate"][0:P])]
            late += [(0, w1[:, e * HID:(e + 1) * HID], t["L0_cond_w1"][e, 0:P, :]) for e in range(E)]
            for k in range(0, CH, CH // 3):
                late.append((0, w2[:, k * C:(k + CH // 3) * C].rearrange("p (k c) -> p k c", c=C),
                             w2f[:, k:k + CH // 3, :]))
            late += [(0, b2bc[:, :, :], t["L0_cond_b2"].partition_broadcast(P)),
                     (1, wqkv[1][:, :], t["L1_cond_w_qkv"][0:P]),
                     (1, wproj[1][:, :], t["L1_cond_w_proj"][0:P]),
                     (1, wfc1[:, :], t["L1_cond_w_fc1"][0:P]),
                     (1, wfc2[:, 0:full, :], t["L1_cond_w_fc2"][0:full * P].rearrange("(k p) c -> p k c", p=P)),
                     (1, wfc2[0:HID - full * P, full, :], t["L1_cond_w_fc2"][full * P:HID]),
                     (1, bfc2[:, :], t["L1_cond_b_fc2"].partition_broadcast(P))]
            assert len(late) == LATE0 + LATE1

            for i, stage in enumerate(SCHED):
                if stage[0] == "qkv":
                    _, l, b = stage
                    n = B * l + b
                    parts = qk_dram[n]
                    main = (HD - 1) * NH
                    for c, w, r, rows, lo in ((0, 0, 0, main, 0), (1, 1, 0, main, 0),
                                              (2, 0, 0, NH, main), (2, 1, NH, NH, main)):
                        sp.wait_ge(qk_split, 3 * n + c + 1)
                        sp.dma_start(parts[w, :, lo:lo + rows, :].rearrange("i r n -> r i n"),
                                     qkp[n][r:r + rows, c, :, :]).then_inc(qk_out[n], 16)
                for n, piece in pieces_after(stage):
                    b, parts = n % B, qk_dram[n]
                    sp.wait_ge(qk_out[n], 4 * 16)
                    if n < B:
                        sp.wait_ge(buf_ready, n + 1)
                    else:
                        sp.wait_ge(t_full, scores_ended(n - B))
                    lo, hi = PIECES[b][piece]
                    width, cols, done = (hi - lo) * N, slice(lo * N, hi * N), qk_in[n][piece]
                    src = parts[1].rearrange("j (d h) n -> (j d) (h n)", h=NH)[:, cols]
                    sp.dma_start(Ks[b][0:PAIRS, lo:hi, :],
                                 src.unsqueeze(0).to_broadcast([PARTS, PARTS * HD, width])).then_inc(done, 16)
                    for i_ in range(PARTS):
                        r = HD * PARTS * i_
                        src = parts[0, i_].rearrange("(d h) n -> d (h n)", h=NH)[:, cols]
                        sp.dma_start(Qs[b][r:r + HD * PARTS, lo:hi, :],
                                     src.unsqueeze(0).to_broadcast([PARTS, HD, width])).then_inc(done, 16)
                if stage[0] == "ada" and stage[1:] != (0, 0):
                    _, l, part = stage
                    sp.wait_ge(t_free, T_AT[i + 1])
                    sp.dma_start(mod_dram[l, part], mod_row[l, part]).then_inc(mod_out, 16)
                    sp.wait_ge(mod_out, 16 * (3 * l + part))
                    sp.dma_start(mod[l][:, :, 2 * part:2 * part + 2, :],
                                 mod_dram[l, part].partition_broadcast(P)).then_inc(mod_in[l][part], 16)
                if stage == ("max", 0, UNIT_LEAD - 1):
                    for l in range(L):
                        for part in range(l == 0, 3):
                            sp.wait_ge(mod_in[l][part], 16)
                if stage[0] == "slot" and late:
                    l, place, source = late.pop(0)
                    sp.dma_start(place, source).then_inc(ld_w[l], 16)
                pair = turns_pair(stage)
                if pair is not None:
                    n, h = 2 * pair // NH, 2 * pair % NH
                    sp.wait_ge(t_free, T_AT[i + 1])
                    if n < B:
                        sp.wait_ge(buf_ready, n + 1)
                    else:
                        sp.wait_ge(t_full, scores_ended(n - B))
                    sp.dma_start(Qs[n % B][MROW:SROWS, h:h + 2, :], mT[:, pair % 2, :]).then_inc(m_in[pair % 4], 16)

        @block.gpsimd
        def _(pool):
            G_ = nc.gpsimd
            sources = {"qkv0": ("L0_cond_w_qkv", "L0_cond_b_qkv"), "proj0": ("L0_cond_w_proj", "L0_cond_b_proj"),
                       "gate": ("L0_cond_w_gate", None), "w1": ("L0_cond_w1", "L0_cond_b1"),
                       "qkv1": ("L1_cond_w_qkv", "L1_cond_b_qkv"), "proj1": ("L1_cond_w_proj", "L1_cond_b_proj"),
                       "fc1": ("L1_cond_w_fc1", "L1_cond_b_fc1")}

            def load_raw(name):
                done = ld_raw[name != "qkv0"]
                w, bias = sources[name]
                a, n = WCOLS[name]
                for rows in STACK.values():
                    lo, k = rows[0][0], len(rows)
                    if name == "w1":
                        for e in range(E):
                            src = t[w][e, P:C, :].unsqueeze(0).to_broadcast([k, CR, HID])
                            pool.dma_start(wraw[lo:lo + k * CR, a + e * HID:a + (e + 1) * HID], src).then_inc(done, 16)
                    else:
                        src = t[w][P:C, :].unsqueeze(0).to_broadcast([k, CR, n])
                        pool.dma_start(wraw[lo:lo + k * CR, a:a + n], src).then_inc(done, 16)
                for r in BIAS_ROWS:
                    if bias is not None:
                        src = t[bias].rearrange("e h -> (e h)") if name == "w1" else t[bias]
                        pool.dma_start(wraw[r:r + 1, a:a + n], src.rearrange("(o n) -> o n", o=1)).then_inc(done, 16)

            step = [0]

            def link(ins):
                step[0] += 1
                ins.then_inc(pool_step, 1)
                pool.wait_ge(pool_step, step[0])

            def split_weights(a, n):
                raw, stk = wraw[:, a:a + n], wstk[:, a:a + n]
                link(G_.tensor_copy(stk, raw))
                link(G_.tensor_scalar(stk, stk, mask1[0:ROWS, 0:1], 0.0, ALU.mult, ALU.add))
                link(G_.tensor_tensor(raw, raw, stk, ALU.add))
                link(G_.tensor_copy(stk, raw))
                link(G_.tensor_scalar(stk, stk, mask2[0:ROWS, 0:1], 0.0, ALU.mult, ALU.add))
                return G_.tensor_tensor(stk, raw, stk, ALU.add)

            load_raw("qkv0")
            G_.memset(mask1[:, :], -1.0)
            G_.memset(mask2[:, :], -1.0)
            G_.memset(ident[:, :], 0.0)
            G_.memset(identb[:, :], 0.0)
            G_.memset(before[:, :, :], 1.0)
            link(G_.memset(wraw[:, WCOLS["gate"][0]:WCOLS["gate"][0] + E], 0.0))
            for m, first in ((mask1, MASK1), (mask2, MASK2)):
                G_.affine_select(out=m[:, :], in_=m[:, :], compare_op=ALU.is_ge, fill=0.0, base=-first,
                                 pattern=[[0, 1]], channel_multiplier=1)
            for m in (ident, identb):
                G_.affine_select(out=m[:, :], in_=m[:, :], compare_op=ALU.not_equal, fill=1.0, base=0,
                                 pattern=[[-1, P]], channel_multiplier=1)
            G_.affine_select(out=before[:, :, :], in_=before[:, :, :], compare_op=ALU.is_gt, fill=0.0, base=0,
                             pattern=[[1, E], [-1, E]], channel_multiplier=0).then_inc(c_ready, 1)
            pool.wait_ge(c_ready, 1)
            pool.wait_ge(ld_raw[0], 16 * 6)
            split_weights(*WCOLS["qkv0"]).then_inc(w_split, 1)
            pool.wait_ge(w_split, 1)
            pair_of_ones = 0x3F803F80
            for b in range(B):
                G_.memset(Qs[b][64:96, :, :].bitcast(I32), 0)
                link(G_.memset(Ks[b][64:96, :, :].bitcast(I32), 0))
                G_.memset(Ks[b][96:SROWS, :, :].bitcast(I32), pair_of_ones).then_inc(buf_ready, 1)
                pool.wait_ge(buf_ready, b + 1)
                if b == 0:
                    link(G_.memset(Va[1][:, :, :, :], 0.0))
                    G_.memset(Va[1][:, :, :, HD:HD + 1], 1.0).then_inc(v_ready[1], 1)
                    pool.wait_ge(v_ready[1], 1)
            for name in sources:
                if name != "qkv0":
                    load_raw(name)
            pool.wait_ge(ld_raw[1], 16 * (5 * 3 + 3 * E + 5 * 3))
            for k, (name, last) in enumerate((("proj0", "gate"), ("w1", "w1"), ("qkv1", "fc1"))):
                a = WCOLS[name][0]
                split_weights(a, sum(WCOLS[last]) - a).then_inc(w_split, 1)

        @block.vector
        def _(dve):
            V = nc.vector
            step = [0]

            def link(ins):
                step[0] += 1
                ins.then_inc(dve_step, 1)
                dve.wait_ge(dve_step, step[0])

            def take(at):
                dve.wait_ge(s_full, at + 1)
                return S_BANKS[at % NS]

            turn_stages = [i for i, stage in enumerate(SCHED) if stage[0] == "turn"]
            prepared = [0]

            def natural_free():
                if prepared[0]:
                    dve.wait_ge(t_full, T_AT[turn_stages[prepared[0] - 1] + 1])
                prepared[0] += 1

            def split_stack(src):
                col = {part: [r for rows in STACK.values() for r, q in rows if q == part] for part in range(PARTS)}
                at = {part: [stN[:, :, r:r + CR] for r in rows] for part, rows in col.items()}
                yield V.tensor_copy(at[0][0], src)
                V.tensor_copy(at[0][1], at[0][0])
                V.tensor_copy(at[0][2], at[0][0])
                yield V.tensor_tensor(rest[:, :, :], src, at[0][0], ALU.subtract)
                yield V.tensor_copy(at[1][0], rest[:, :, :])
                yield V.tensor_copy(at[1][1], at[1][0])
                V.tensor_tensor(at[2][0], rest[:, :, :], at[1][0], ALU.subtract).then_inc(nat_ready, 1)

            def heads_innermost(l):
                a = WCOLS[f"qkv{l}"][0]
                for src, dst in ((wqkv[l][:, :], wqk[l][:, :]), (wstk[:, a:a + 3 * C], wqk_stk[l][:, :])):
                    for w in range(2):
                        ins = V.tensor_copy(dst[:, w * P:(w + 1) * P].rearrange("p (d h) -> p d h", h=NH),
                                      src[:, w * C:(w + 1) * C].rearrange("p (h d) -> p d h", d=HD)[:, 0:HD - 1, :])
                    ins = V.tensor_copy(dst[:, 2 * P:2 * C], src[:, HD - 1:2 * C:HD])
                ins.then_inc(w_ready, 1)

            def norm_stats(bs):
                for b in range(B)[bs]:
                    for k in range(NT):
                        ins = V.bn_stats(stats[:, b, k, :], x[:, b, k, :])
                yield ins
                for b in range(B)[bs]:
                    for k in range(NT):
                        ins = V.bn_aggr(mv[:, b, k, :], stats[:, b, k, :])
                yield ins
                yield V.tensor_scalar(var[:, bs, :], mv[:, bs, :, 1], EPS, None, ALU.add)
                r, bits = rs[:, bs, :], rs[:, bs, :].bitcast(I32)
                yield V.tensor_single_scalar(bits, var[:, bs, :].bitcast(I32), 1, ALU.arith_shift_right)
                yield V.tensor_scalar(bits, bits, -1.0, float(0x5F3759DF), ALU.mult, ALU.add)
                for _ in range(3):
                    yield V.tensor_tensor(nw[:, bs, 0, :], r, r, ALU.mult)
                    yield V.scalar_tensor_tensor(nw[:, bs, 1, :], nw[:, bs, 0, :], -0.5, var[:, bs, :],
                                                 ALU.mult, ALU.mult)
                    yield V.scalar_tensor_tensor(r, nw[:, bs, 1, :], 1.5, r, ALU.add, ALU.mult)

            def norm_apply(l, b, shift, scale):
                natural_free()
                for k in range(NT):
                    ins = V.scalar_tensor_tensor(hN[:, k, :], x[:, b, k, :], mv[:, b, k, 0:1], mod[l][:, b, scale, :],
                                                 ALU.subtract, ALU.mult)
                yield ins
                for k in range(NT):
                    ins = V.scalar_tensor_tensor(hN[:, k, :], hN[:, k, :], rs[:, b, k:k + 1], mod[l][:, b, shift, :],
                                                 ALU.mult, ALU.add)
                yield ins
                yield from split_stack(hN[:, :, P:C])

            waiting = []

            def advance():
                while waiting:
                    gen, last = waiting[0]
                    if last is not None:
                        dve.wait_ge(dve_step, last)
                    ins = next(gen, None)
                    if ins is not None:
                        step[0] += 1
                        ins.then_inc(dve_step, 1)
                        waiting[0] = (gen, step[0])
                        return
                    waiting.pop(0)

            def finish():
                while waiting:
                    advance()

            def run(gen):
                finish()
                waiting.append((gen, None))
                finish()

            def split_max_first(pair, s_at):
                if pair >= 2:
                    dve.wait_ge(t_full, pair_turned(pair - 2))
                dve.wait_ge(s_free, s_at)
                V.tensor_copy(mpart[:, pair % 2, 0, :], nmax[:, pair % 2, :]).then_inc(m_first, 1)

            def split_max_second(pair):
                dve.wait_ge(m_first, pair + 1)
                V.tensor_tensor(mpart[:, pair % 2, 1, :], nmax[:, pair % 2, :], mpart[:, pair % 2, 0, :],
                                ALU.subtract).then_inc(m_split, 1)

            def gate_rows(l, b, gate, tiles):
                return mod[l][:, b, gate, :].unsqueeze(1).to_broadcast([P, tiles, C])

            for r in BIAS_ROWS:
                V.memset(stN[:, :, r:r + 1], 1.0)
            V.memset(ones[:, :], 1.0)
            V.memset(siluBr[:, :, :], 1.0)
            link(V.memset(Va[0][:, :, :, :], 0.0))
            V.memset(Va[0][:, :, :, HD:HD + 1], 1.0).then_inc(v_ready[0], 1)

            for i, stage in enumerate(SCHED):
                kind, s_at = stage[0], S_AT[i]
                if kind == "ada":
                    if stage[1:] == (0, 0):
                        dve.wait_ge(silu_exp, 2)
                        V.tensor_scalar(ex[:, :], ex[:, :], 1.0, None, ALU.add)
                        link(V.tensor_scalar(exr[:, :], exr[:, :], 1.0, None, ALU.add))
                        V.reciprocal(ex[:, :], ex[:, :])
                        link(V.reciprocal(exr[:, :], exr[:, :]))
                        V.tensor_tensor(cT[:, :], cT[:, :], ex[:, :], ALU.mult)
                        link(V.tensor_tensor(cTr[:, :], cTr[:, :], exr[:, :], ALU.mult))
                        for b in range(B):
                            V.tensor_scalar(siluB[:, b, :], ones[:, :], cT[:, b:b + 1], None, ALU.mult)
                            ins = V.tensor_scalar(siluBr[0:CR, b, :], ones[0:CR, :], cTr[:, b:b + 1], None, ALU.mult)
                        ins.then_inc(silu_done, 1)
                elif kind == "lnstat":
                    for b in range(B):
                        dve.wait_ge(ld_x[b], 16)
                    run(norm_stats(slice(0, B)))
                elif kind == "ln":
                    _, l, which = stage
                    b = which % B
                    if l == 0 and which < B:
                        dve.wait_ge(t_free, T_AT[WHERE[("ada", 0, 0)] + 1])
                    else:
                        for part in range(3):
                            if l or part:
                                dve.wait_ge(mod_in[l][part], 16)
                        waiting.append((norm_stats(slice(b, b + 1)), None))
                    waiting.append((norm_apply(l, b, 3 * (which // B), 3 * (which // B) + 1), None))
                elif kind == "turn":
                    finish()
                    if prepared[0] == 1:
                        dve.wait_ge(ld_qkv, 16)
                        dve.wait_ge(w_split, 1)
                        heads_innermost(0)
                elif kind == "qkv":
                    _, l, b = stage
                    n = B * l + b
                    finish()
                    f, q = qkf[n], qkp[n]
                    made = [0] * 3
                    for part in range(PARTS):
                        for c, rows in ((0, P), (1, P), (2, 2 * NH)):
                            if part == 0:
                                dve.wait_ge(t_free, T_AT[i] + c + 1)
                                ins = V.tensor_tensor(f[0:rows, c, :], f[0:rows, c, :], q[0:rows, c, 0, :], ALU.subtract)
                            else:
                                dve.wait_ge(dve_step, made[c])
                                if part == 1:
                                    ins = V.tensor_copy(q[0:rows, c, 1, :], f[0:rows, c, :])
                                else:
                                    V.tensor_tensor(q[0:rows, c, 2, :], f[0:rows, c, :], q[0:rows, c, 1, :],
                                                    ALU.subtract).then_inc(qk_split, 1)
                                    continue
                            step[0] += 1
                            ins.then_inc(dve_step, 1)
                            made[c] = step[0]
                elif kind == "osplit":
                    _, l, b = stage
                    finish()
                    natural_free()
                    run(split_stack(oN[b][:, :, P:C]))
                elif kind == "proj":
                    _, l, b = stage
                    dve.wait_ge(mod_in[l][1], 16)
                    for k in range(NT // 2):
                        bank = take(s_at + k)
                        V.tensor_tensor(attn[:, 2 * k:2 * k + 2, :], bank[:, 0:2 * C].rearrange("p (t c) -> p t c", t=2),
                                        gate_rows(l, b, 2, 2), ALU.mult).then_inc(s_free, 1)
                    dve.wait_ge(s_free, s_at + NT // 2)
                    link(V.tensor_tensor(x[:, b], x[:, b], attn[:, :, :], ALU.add))
                elif kind == "gate":
                    b = stage[1]
                    bank = take(s_at)
                    V.tensor_copy(lg[:, :, :], bank[:, 0:NT * E].rearrange("p (t e) -> p t e", e=E)).then_inc(s_free, 1)
                    dve.wait_ge(s_free, s_at + 1)
                    me = lg[:, :, :].unsqueeze(3).to_broadcast([P, NT, E, E])
                    other = lg[:, :, :].unsqueeze(2).to_broadcast([P, NT, E, E])
                    V.tensor_tensor(cmp[:, 0], other, me, ALU.is_gt)
                    V.tensor_tensor(cmp[:, 1], other, me, ALU.is_equal)
                    link(V.tensor_reduce(gmax[:, :], lg[:, :, :], AX.X, ALU.max))
                    V.tensor_tensor(lg[:, :, :], lg[:, :, :], gmax[:, :].unsqueeze(2).to_broadcast([P, NT, E]),
                                    ALU.subtract).then_inc(logit_ready, 1)
                    early = before[:, :, :].unsqueeze(1).to_broadcast([P, NT, E, E])
                    link(V.tensor_tensor(cmp[:, 1], cmp[:, 1], early, ALU.mult))
                    link(V.tensor_tensor(cmp[:, 0], cmp[:, 0], cmp[:, 1], ALU.add))
                    link(V.tensor_reduce(rank[:, :, :], cmp[:, 0], AX.X, ALU.add))
                    dve.wait_ge(gate_exp, b + 1)
                    link(V.scalar_tensor_tensor(gex[:, :, :], rank[:, :, :], 2.0, gex[:, :, :], ALU.is_lt, ALU.mult))
                    link(V.tensor_reduce(gsum[:, :], gex[:, :, :], AX.X, ALU.add))
                    link(V.reciprocal(gsum[:, :], gsum[:, :]))
                    V.tensor_tensor(cw[b][:, :, :], gex[:, :, :], gsum[:, :].unsqueeze(2).to_broadcast([P, NT, E]),
                                    ALU.mult).then_inc(cw_ready, 1)
                elif stage == ("fc1", 0, 1, 0, CHH):
                    dve.wait_ge(ld_w[1], 16 * LATE1)
                    dve.wait_ge(w_split, 4)
                    heads_innermost(1)
                elif kind == "fc2":
                    _, b, half, e2 = stage
                    if half == 0 and e2 == 0:
                        dve.wait_ge(cw_ready, b + 1)
                        dve.wait_ge(ld_w[0], 16 * LATE0)
                        finish()
                        for e in range(E):
                            for k in range(NT):
                                if e == 0:
                                    ins = V.tensor_scalar(y[:, k, :], b2bc[:, 0, :], cw[b][:, k, 0:1], None, ALU.mult)
                                else:
                                    ins = V.scalar_tensor_tensor(y[:, k, :], b2bc[:, e, :], cw[b][:, k, e:e + 1],
                                                                 y[:, k, :], ALU.mult, ALU.add)
                            link(ins)
                    e = E2 * half + e2
                    dve.wait_ge(s_free, s_at)
                    for k in range(NT):
                        bank = take(s_at + k)
                        V.scalar_tensor_tensor(y[:, k, :], bank[:, 0:C], cw[b][:, k, e:e + 1], y[:, k, :],
                                               ALU.mult, ALU.add).then_inc(s_free, 1)
                        advance()
                    dve.wait_ge(s_free, S_AT[i + 1])
                    if half and e2:
                        link(V.tensor_tensor(y[:, :, :], y[:, :, :], gate_rows(0, b, 5, NT), ALU.mult))
                        link(V.tensor_tensor(x[:, b], x[:, b], y[:, :, :], ALU.add))
                elif kind == "mlp2":
                    b = stage[1]
                    if b:
                        dve.wait_ge(x_ready, b)
                    for k in range(NT):
                        bank = take(s_at + k)
                        V.tensor_tensor(y[:, k, :], bank[:, 0:C], bfc2[:, :], ALU.add).then_inc(s_free, 1)
                        advance()
                    dve.wait_ge(s_free, S_AT[i + 1])
                    link(V.tensor_tensor(y[:, :, :], y[:, :, :], gate_rows(1, b, 5, NT), ALU.mult))
                    V.tensor_tensor(x[:, b], x[:, b], y[:, :, :], ALU.add).then_inc(x_ready, 1)

                u = unit_of(stage)
                if u is not None:
                    pair, odd = (NH * stage[1] + u) // 2, u % 2
                    half = pair % 2
                    for k in range(NT):
                        bank = take(s_at + k)
                        V.tensor_reduce(nmax[:, half, odd * NT + k:odd * NT + k + 1], bank[:, :], AX.X, ALU.max,
                                        negate=True).then_inc(s_free, 1)
                        if k == 0 and not odd and u:
                            split_max_first(pair - 1, s_at)
                        elif k == 1 and not odd and u:
                            split_max_second(pair - 1)
                        else:
                            advance()
                if turns_pair(stage) is not None and u is None:
                    split_max_first(turns_pair(stage), s_at)
                    split_max_second(turns_pair(stage))
                g, k = finishes(stage)
                if k == 2:
                    b, hg = g // HG, g % HG
                    at = S_AT[i + 1] - 1
                    o = take(at)[:, :].rearrange("p (t g w) -> p t g w", t=NT, g=G)
                    link(V.reciprocal(rec[:, :, :], o[:, :, :, HD]))
                    dst = oN[b][:, :, hg * G * HD:(hg + 1) * G * HD].rearrange("p t (g d) -> p t g d", d=HD)
                    V.tensor_tensor(dst, o[:, :, :, 0:HD], rec[:, :, :].unsqueeze(3).to_broadcast([P, NT, G, HD]),
                                    ALU.mult).then_inc(s_free, 1)
                    dve.wait_ge(s_free, at + 1)

        @block.scalar
        def _(act):
            A = nc.scalar
            last_use = {}

            def take(at):
                act.wait_ge(t_full, at + 1)
                return T_BANKS[at % NTB]

            act.dma_start(cT[:, :], t["cond_1152"][:, 0:P].rearrange("b c -> c b"),
                          allow_slow_non_contiguous=True).then_inc(ld_c, 16)
            act.dma_start(cTr[:, :], t["cond_1152"][:, P:C].rearrange("b c -> c b"),
                          allow_slow_non_contiguous=True).then_inc(ld_c, 16)

            for i, stage in enumerate(SCHED):
                kind, t_at = stage[0], T_AT[i]
                if kind == "ada":
                    _, l, part = stage
                    if stage[1:] == (0, 0):
                        act.wait_ge(ld_c, 32)
                        A.activation(ex[:, :], cT[:, :], ACT.Exp, scale=-1.0).then_inc(silu_exp, 1)
                        A.activation(exr[:, :], cTr[:, :], ACT.Exp, scale=-1.0).then_inc(silu_exp, 1)
                    for j in range(B if stage[1:] == (0, 0) else 1):
                        bank = take(t_at + j)
                        for r in range(2):
                            bias = 1.0 if 2 * part + r in (1, 4) else 0.0
                            cols = slice(r * C, (r + 1) * C)
                            if stage[1:] == (0, 0):
                                ins = A.activation(mod[0][:, j, r, :], bank[:, cols], ACT.Copy, bias=bias)
                            else:
                                ins = A.activation(mod_row[l, part][:, r, :], bank[0:B, cols], ACT.Copy, bias=bias)
                        ins.then_inc(t_free, 1)
                elif kind == "turn":
                    _, l, b, buf = stage
                    key = buf if buf == "a" else (buf, b)
                    if key in last_use:
                        j = last_use[key]
                        if SCHED[j][0] == "proj":
                            act.wait_ge(s_full, S_AT[j + 1])
                        else:
                            act.wait_ge(t_full, T_AT[j + 1])
                    last_use[key] = tile_used(i)
                    bank = take(t_at)
                    A.activation(hT[buf][b][:, :], bank[:, :], ACT.Copy).then_inc(t_free, 1)
                    bank = take(t_at + 1)
                    A.activation(hS[buf][b][:, :], bank[0:ROWS, 0:N // 2].bitcast(BF16), ACT.Copy).then_inc(t_free, 1)
                elif kind == "qkv":
                    _, l, b = stage
                    n = B * l + b
                    if n:
                        act.wait_ge(qk_out[n - 1], 4 * 16)
                    if n == B:
                        act.wait_ge(p_used, NT * B * HG)
                    if n == B + 1:
                        act.wait_ge(s_full, S_AT[WHERE[("fc2", 1, 1, 1)] + 1])
                    for c, rows in ((0, P), (1, P), (2, 2 * NH)):
                        bank = take(t_at + c)
                        A.activation(qkf[n][0:rows, c, :], bank[0:rows, :], ACT.Copy)
                        A.activation(qkp[n][0:rows, c, 0, :], bank[0:rows, :], ACT.Copy).then_inc(t_free, 1)
                    if n < B:
                        act.wait_ge(v_ready[n], 1)
                    else:
                        act.wait_ge(p_used, NT * HG * (n - 1))
                    for k in range(NT // 2):
                        bank = take(t_at + 3 + k)
                        A.activation(Va[b][:, 2 * k:2 * k + 2, :, 0:HD],
                                     bank[:, 0:2 * C].rearrange("p (t h d) -> p t h d", t=2, d=HD),
                                     ACT.Copy).then_inc(t_free, 1)
                elif kind == "gate":
                    b = stage[1]
                    act.wait_ge(logit_ready, b + 1)
                    if b:
                        act.wait_ge(cw_ready, b)
                    A.activation(gex[:, :, :], lg[:, :, :], ACT.Exp).then_inc(gate_exp, 1)
                elif kind in ("fc1", "mlp1"):
                    lo, hi = stage[3:5] if kind == "fc1" else (0, CH1)
                    prev = [j for j in range(i) if SCHED[j][0] in ("fc2", "mlp2")]
                    if prev and lo == 0:
                        act.wait_ge(s_full, S_AT[prev[-1] + 1])
                    if stage == ("mlp1", 0):
                        act.wait_ge(qk_out[B * L - 1], 4 * 16)
                    if kind == "fc1" and stage[1:] == (0, 0, 0, 5):
                        act.wait_ge(w_split, 4)
                    for c in range(lo, hi):
                        rows = P if kind == "fc1" else min(P, HID - c * P)
                        bank = take(t_at + c - lo)
                        A.activation(hmid[0:rows, c, :], bank[0:rows, :], ACT.Gelu_apprx_tanh).then_inc(t_free, 1)
                if kind == "slot":
                    _, n0, g, k = stage
                    done = NT * (HG * n0 + g) + k
                    if g == 0 and k == 0:
                        act.wait_ge(qk_out[1 if n0 == 0 else B], 4 * 16)
                    for j in range(G):
                        bank = take(t_at + j)
                        if done >= 2 and j == 0:
                            act.wait_ge(p_used, done - 1)
                        A.activation(probs[:, k % 2, j, :], bank[:, :], ACT.Exp, scale=SCALE).then_inc(t_free, 1)
                pair = turns_pair(stage)
                if pair is not None:
                    if pair >= 2:
                        act.wait_ge(m_in[(pair - 2) % 4], 16 * ((pair - 2) // 4 + 1))
                    bank = take(T_AT[i + 1] - 1)
                    A.activation(mT[:, pair % 2, :], bank[0:MPARTS * 2 * NT, 0:P // 2].bitcast(BF16), ACT.Copy)\
                        .then_inc(t_free, 1)
                g, k = finishes(stage)
                if k == 1:
                    gn = HG * stage[1] + g
                    act.wait_ge(p_used, NT * (gn + 1))
                    if gn >= 2:
                        act.wait_ge(s_full, turned_back(gn - 2))
                    A.activation(oT[:, gn % 2, :], O_BANKS[gn % 2][:, :], ACT.Copy).then_inc(o_copied, 1)
            for b in range(B):
                act.wait_ge(x_ready, b + 1)
                act.dma_start(out[b].rearrange("(t p) c -> p t c", p=P), x[:, b]).then_inc(stored, 16)
            act.wait_ge(stored, 16 * B)

        @block.tensor
        def _(pe):
            M = nc.tensor
            turns = [0]
            from_attention = set()

            def fill_s(at):
                if at >= NS:
                    pe.wait_ge(s_free, at - NS + 1)
                return S_BANKS[at % NS]

            def fill_t(at):
                if at >= NTB:
                    pe.wait_ge(t_free, at - NTB + 1)
                return T_BANKS[at % NTB]

            def stacked(name, lo, hi):
                a, _ = WCOLS[name]
                return wstk[:, a + lo:a + hi]

            def second(n0, g, k):
                gn = HG * n0 + g
                b, h0 = g // HG, G * (g % HG)
                if k == 0 and gn >= 2:
                    pe.wait_ge(o_copied, gn - 1)
                pe.wait_ge(t_free, T_AT[WHERE[("slot", n0, g, k)]] + G)
                for j in range(G):
                    ins = M.matmul(O_BANKS[gn % 2][OW * j:OW * (j + 1), :], Va[b][:, k, h0 + j, :],
                                   probs[:, k % 2, j, :], start=(k == 0), stop=(k == NT - 1), skip_group_check=True)
                ins.then_inc(p_used, 1)

            for i, stage in enumerate(SCHED):
                kind, s_at, t_at = stage[0], S_AT[i], T_AT[i]
                if kind == "ada":
                    _, l, part = stage
                    pe.wait_ge(silu_done, 1)
                    pe.wait_ge(ld_ada[l], 48)
                    cols = slice(2 * C * part, 2 * C * (part + 1))
                    outs = [(P, siluB[:, b, :], siluBr[:, b, :]) for b in range(B)]
                    if stage[1:] != (0, 0):
                        outs = [(B, siluB[:, :, 0], siluBr[:, :, 0])]
                    for j, (rows, main, others) in enumerate(outs):
                        bank = fill_t(t_at + j)
                        M.matmul(bank[0:rows, 0:2 * C], main, wada[l][:, cols], start=True, stop=False)
                        M.matmul(bank[0:rows, 0:2 * C], others, wadar[l][:, cols], start=False, stop=True)\
                            .then_inc(t_full, 1)
                elif kind == "turn":
                    _, l, b, buf = stage
                    turns[0] += 1
                    if turns[0] == 1:
                        pe.wait_ge(c_ready, 1)
                    pe.wait_ge(nat_ready, turns[0])
                    src = oN[b] if (l, b, buf) in from_attention else hN
                    from_attention.add((l, b, "a"))
                    bank = fill_t(t_at)
                    for k in range(NT):
                        ins = M.transpose(bank[:, k * P:(k + 1) * P], src[:, k, 0:P], ident[:, :])
                    ins.then_inc(t_full, 1)
                    view = fill_t(t_at + 1)[0:ROWS, 0:N // 2].bitcast(BF16)
                    for k in range(NT):
                        ins = M.transpose(view[:, k * P:(k + 1) * P], stN[:, k, 0:ROWS], identb[:, :])
                    ins.then_inc(t_full, 1)
                elif kind == "qkv":
                    _, l, b = stage
                    h, s = hT["a"][b], hS["a"][b]
                    pe.wait_ge(t_free, t_at)
                    pe.wait_ge(w_ready, 1 + l)
                    pe.wait_ge(*((ld_qkv, 16) if l == 0 else (ld_w[1], 16 * LATE1)))
                    name = f"qkv{l}"

                    for c, lo, cols in ((0, 0, P), (1, P, P), (2, 2 * P, 2 * NH)):
                        bank = fill_t(t_at + c)
                        M.matmul(bank[0:cols, :], wqk[l][:, lo:lo + cols], h[:, :], start=True, stop=False)
                        M.matmul(bank[0:cols, :], wqk_stk[l][:, lo:lo + cols], s[:, :],
                                 start=False, stop=True).then_inc(t_full, 1)
                    for k2 in range(NT // 2):
                        bank = fill_t(t_at + 3 + k2)
                        for k in range(2):
                            at = slice((2 * k2 + k) * P, (2 * k2 + k + 1) * P)
                            M.matmul(bank[:, k * C:(k + 1) * C], h[:, at], wqkv[l][:, 2 * C:3 * C],
                                     start=True, stop=False)
                            ins = M.matmul(bank[:, k * C:(k + 1) * C], s[:, at], stacked(name, 2 * C, 3 * C),
                                           start=False, stop=True)
                        ins.then_inc(t_full, 1)
                elif kind == "proj":
                    _, l, b = stage
                    h, s = hT["a"][b], hS["a"][b]
                    pe.wait_ge(t_free, t_at)
                    pe.wait_ge(w_split, 2 if l == 0 else 4)
                    pe.wait_ge(ld_w[l], 16 * (LATE1 if l else LATE0))
                    for k2 in range(NT // 2):
                        bank = fill_s(s_at + k2)
                        for k in range(2):
                            at = slice((2 * k2 + k) * P, (2 * k2 + k + 1) * P)
                            M.matmul(bank[:, k * C:(k + 1) * C], h[:, at], wproj[l][:, :], start=True, stop=False)
                            ins = M.matmul(bank[:, k * C:(k + 1) * C], s[:, at], stacked(f"proj{l}", 0, C),
                                           start=False, stop=True)
                        ins.then_inc(s_full, 1)
                elif kind == "gate":
                    b = stage[1]
                    h, s = hT["b"][b], hS["b"][b]
                    pe.wait_ge(t_free, t_at)
                    bank = fill_s(s_at)
                    for k in range(NT):
                        at = slice(k * P, (k + 1) * P)
                        M.matmul(bank[:, k * E:(k + 1) * E], h[:, at], wgate[:, :], start=True, stop=False)
                        ins = M.matmul(bank[:, k * E:(k + 1) * E], s[:, at], stacked("gate", 0, E),
                                       start=False, stop=True)
                    ins.then_inc(s_full, 1)
                elif kind in ("fc1", "mlp1"):
                    b = stage[1]
                    h, s = hT["b"][b], hS["b"][b]
                    name, w, base = ("w1", w1, CHH * stage[2]) if kind == "fc1" else ("fc1", wfc1, 0)
                    first, last = stage[3:5] if kind == "fc1" else (0, CH1)
                    pe.wait_ge(w_split, 3 if kind == "fc1" else 4)
                    pe.wait_ge(t_free, T_AT[WHERE[("turn", 0 if kind == "fc1" else 1, b, "b")] + 1])
                    for c in range(first, last):
                        rows = P if kind == "fc1" else min(P, HID - c * P)
                        lo = (base + c) * P
                        bank = fill_t(t_at + c - first)
                        M.matmul(bank[0:rows, :], w[:, lo:lo + rows], h[:, :], start=True, stop=False)
                        M.matmul(bank[0:rows, :], stacked(name, lo, lo + rows), s[:, :], start=False, stop=True)\
                            .then_inc(t_full, 1)
                elif kind in ("fc2", "mlp2"):
                    b = stage[1]
                    made = max(j for j in range(i) if SCHED[j][0] == ("fc1" if kind == "fc2" else "mlp1"))
                    pe.wait_ge(t_free, T_AT[made + 1])
                    for e in [stage[3]] if kind == "fc2" else [0]:
                        for k in range(NT):
                            bank = fill_s(s_at + k)
                            if kind == "fc2":
                                parts = hidden_parts(e)
                            else:
                                parts = [(c, 0, min(P, HID - c * P)) for c in range(CH1)]
                            for c, lo, hi in parts:
                                if kind == "fc2":
                                    chunk = CHH * stage[2] + c
                                    w = w2[lo:hi, chunk * C:(chunk + 1) * C]
                                else:
                                    w = wfc2[lo:hi, c, :]
                                ins = M.matmul(bank[:, 0:C], hmid[lo:hi, c, k * P:(k + 1) * P], w,
                                               start=(c == parts[0][0]), stop=(c == parts[-1][0]))
                            ins.then_inc(s_full, 1)

                u = unit_of(stage)
                for k4 in range(NT):
                    if u is not None:
                        n, h_ = stage[1] + u // NH, u % NH
                        b = n % B
                        for piece, (lo, _) in enumerate(PIECES[b]):
                            if k4 == 0 and h_ == lo:
                                pe.wait_ge(qk_in[n][piece], 16 * (1 + PARTS))
                        bank = fill_s(s_at + k4)
                        M.matmul(bank[:, :], Qs[b][0:MROW, h_, k4 * P:(k4 + 1) * P], Ks[b][0:MROW, h_, :],
                                 start=True, stop=True).then_inc(s_full, 1)
                    if kind == "slot":
                        _, n0, g, k = stage
                        b, h0 = g // HG, G * (g % HG)
                        if k == 0 and k4 % 2 == 0:
                            pair = (NH * n0 + G * g + k4) // 2
                            pe.wait_ge(m_in[pair % 4], 16 * (pair // 4 + 1))
                        bank = fill_t(t_at + k4)
                        M.matmul(bank[:, :], Ks[b][0:SROWS, h0 + k4, k * P:(k + 1) * P], Qs[b][0:SROWS, h0 + k4, :],
                                 start=True, stop=True).then_inc(t_full, 1)
                if kind == "slot" and (g or k):
                    second(n0, *((g, k - 1) if k else (g - 1, NT - 1)))
                if kind == "tail" and stage[2] == 0:
                    second(stage[1], B * HG - 1, NT - 1)
                pair = turns_pair(stage)
                if pair is not None:
                    pe.wait_ge(m_split, pair + 1)
                    view = fill_t(T_AT[i + 1] - 1)[0:MPARTS * 2 * NT, 0:P // 2].bitcast(BF16)
                    M.transpose(view, mpart[:, pair % 2, :, :].rearrange("p i k -> p (i k)"), identb[:, :])\
                        .then_inc(t_full, 1)
                g, k = finishes(stage)
                if k == 2:
                    gn = HG * stage[1] + g
                    pe.wait_ge(o_copied, gn + 1)
                    bank = fill_s(S_AT[i + 1] - 1)
                    for q in range(NT):
                        ins = M.transpose(bank[:, q * P:(q + 1) * P], oT[:, gn % 2, q * P:(q + 1) * P], ident[:, :])
                    ins.then_inc(s_full, 1)


def kernel(**inputs):
    import numpy as _np
    import concourse.bacc as _bacc
    from concourse import mybir as _mybir
    from concourse.bass_utils import run_bass_kernel_spmd as _run

    nc = _bacc.Bacc("TRN2", target_bir_lowering=False, num_devices=1)
    arrays, args = {}, {}
    for name, value in inputs.items():
        a = _np.ascontiguousarray(value)
        arrays[f"in_{name}_dram"] = a
        args[name] = nc.dram_tensor(f"in_{name}_dram", a.shape, _mybir.dt.from_np(a.dtype),
                                    kind="ExternalInput").ap()
    out = nc.dram_tensor("out_0_dram", (B, N, C), F32, kind="ExternalOutput").ap()
    build(nc, args, out)
    r = _run(nc, [arrays], core_ids=[0])
    return r.results[0]["out_0_dram"]
```

```python
from contextlib import ExitStack

import concourse.bass as bass
from concourse import mybir

F32 = mybir.dt.float32
BF16 = mybir.dt.bfloat16
I32 = mybir.dt.int32
ALU = mybir.AluOpType
ACT = mybir.ActivationFunctionType
AX = mybir.AxisListType

P = 128
B, N, C = 2, 512, 144
NT = N // P
NH, HD = 16, 9
CR = C - P
E, HID = 4, 4 * C
CH = E * HID // P
E2 = E // 2
CHH = CH // 2
CH1 = -(-HID // P)
QKV = 3 + NT // 2
L = 2
EPS = 1e-6
SCALE = HD ** -0.5
PARTS = 3
PAIRS = PARTS * PARTS * HD
MROW = 96
MPARTS = 2
SROWS = MROW + MPARTS
G = 4
HG = NH // G
UNIT_LEAD = 6
OW = 32

STACK = {0: ((0, 2), (16, 1), (32, 0)), 1: ((49, 1), (65, 0)), 2: ((82, 0),)}
BIAS_ROWS = (48, 81, 98)
ROWS = 99
MASK1, MASK2 = 49, 82

WCOLS = {}
_at = 0
for _name, _n in (("qkv0", 3 * C), ("proj0", C), ("gate", E), ("w1", E * HID),
                  ("qkv1", 3 * C), ("proj1", C), ("fc1", HID)):
    WCOLS[_name] = (_at, _n)
    _at += _n
WN = _at


def schedule():
    s = [("ada", 0, 0), ("ln", 0, 0), ("ada", 0, 1), ("ada", 0, 2), ("turn", 0, 0, "a"), ("ln", 0, 1),
         ("qkv", 0, 0, 0, QKV), ("turn", 0, 1, "a"), ("ada", 1, 0), ("ada", 1, 1), ("qkv", 0, 1, 0, QKV), ("ada", 1, 2)]
    s += [("max", 0, u) for u in range(UNIT_LEAD)]
    for l in range(L):
        n0 = B * l
        after = {(4, 3): [("osplit", l, 0)], (5, 0): [("turn", l, 0, "a")], (5, 2): [("proj", l, 0), ("ln", l, 2)],
                 (7, 0): [("turn", l, 0, "b")]}
        if l == 0:
            after[7, 1] = [("gate", 0)]
        else:
            after[0, 3] = [("turn", l, 1, "a")]
            after[1, 0] = [("qkv", l, 1, 0, 1)]
            after[1, 1] = [("qkv", l, 1, 1, 2)]
            after[1, 2] = [("qkv", l, 1, 2, 3)]
            after[1, 3] = [("qkv", l, 1, 3, QKV)]
        for g in range(B * HG):
            for k in range(NT):
                s += [("slot", n0, g, k)] + after.get((g, k), [])
        s += [("tail", n0, 0), ("tail", n0, 1), ("tail", n0, 2), ("osplit", l, 1)]
        if l == 0:
            s += [("fc1", 0, 0, 0, CHH), ("turn", 0, 1, "a"), ("fc2", 0, 0, 0, 0, NT), ("proj", 0, 1), ("ln", 0, 3),
                  ("fc2", 0, 0, 1, 0, NT), ("fc1", 0, 1, 0, CHH), ("turn", 0, 1, "b"), ("fc2", 0, 1, 0, 0, NT),
                  ("gate", 1), ("fc2", 0, 1, 1, 0, NT)]
            s += [("ln", 1, 0), ("fc1", 1, 0, 0, CHH), ("turn", 1, 0, "a"), ("fc2", 1, 0, 0, 0, NT),
                  ("qkv", 1, 0, 0, QKV), ("fc2", 1, 0, 1, 0, NT), ("fc1", 1, 1, 0, 5), ("max", B, 0),
                  ("fc1", 1, 1, 5, 7), ("max", B, 1), ("fc1", 1, 1, 7, CHH)]
            for j in range(2 * NT):
                s += [("max", B, 2 + j // 2, j % 2 * NT // 2, (j % 2 + 1) * NT // 2),
                      ("fc2", 1, 1, j // NT, j % NT, j % NT + 1)]
            s += [("ln", 1, 1)]
        else:
            s += [("mlp1", 0, 0, 0, 1), ("turn", 1, 1, "a"), ("proj", 1, 1), ("ln", 1, 3), ("mlp1", 0, 0, 1, CH1),
                  ("mlp2", 0), ("turn", 1, 1, "b"), ("mlp1", 1, 0, 0, CH1), ("mlp2", 1)]
    return s


SCHED = schedule()
LATE0, LATE1 = 10, 6


PIECES = (((0, G), (G, NH)), tuple((h, h + G) for h in range(0, NH, G)))
PIECES_AT = (((0, 1), (0, 3), (1, 1), (1, 3)), ((2, 0), (2, 1), (2, 3), (3, 1)))


def pieces_after(stage):
    if stage[0] == "qkv" and stage[2] == 0 and stage[4] == QKV:
        return [(B * stage[1], piece) for piece in range(len(PIECES[0]))]
    if stage[0] == "slot" and stage[2:] in PIECES_AT[stage[1] // B]:
        return [(stage[1] + 1, PIECES_AT[stage[1] // B].index(stage[2:]))]
    return []


def unit_of(stage):
    u = stage[2] if stage[0] == "max" else NT * stage[2] + stage[3] + UNIT_LEAD if stage[0] == "slot" else None
    return u if u is not None and u < B * NH else None


def tiles_of(stage):
    return stage[3:5] if stage[0] == "max" and len(stage) > 3 else (0, NT)


def turns_pair(stage):
    if stage[0] not in ("max", "slot") or tiles_of(stage)[1] < NT:
        return None
    u = stage[2] if stage[0] == "max" else NT * stage[2] + stage[3] + UNIT_LEAD
    return (NH * stage[1] + u) // 2 - 1 if u % 2 == 0 and 2 <= u <= B * NH else None


def finishes(stage):
    if stage[0] == "slot" and stage[2]:
        return stage[2] - 1, stage[3]
    if stage[0] == "tail":
        return B * HG - 1, stage[2]
    return None, None


def banks_used(stage):
    kind, s, t = stage[0], 0, 0
    if kind == "ada":
        t = B if stage[1:] == (0, 0) else 1
    elif kind == "turn":
        t = 2
    elif kind == "qkv":
        t = stage[4] - stage[3]
    elif kind == "proj":
        s = NT // 2
    elif kind == "gate":
        s = 1
    elif kind in ("fc1", "mlp1"):
        t = stage[4] - stage[3]
    elif kind == "fc2":
        s = stage[5] - stage[4]
    elif kind == "mlp2":
        s = NT
    if kind == "slot":
        t += G
    u = unit_of(stage)
    if u is not None:
        s += tiles_of(stage)[1] - tiles_of(stage)[0]
    if turns_pair(stage) is not None:
        t += 1
    if finishes(stage)[1] == 2:
        s += 1
    return s, t


S_AT, T_AT = [0], [0]
for _stage in SCHED:
    _s, _t = banks_used(_stage)
    S_AT.append(S_AT[-1] + _s)
    T_AT.append(T_AT[-1] + _t)
WHERE = {}
for _i, _stage in enumerate(SCHED):
    WHERE[_stage] = _i


PAIR_STAGE = [i for i, stage in enumerate(SCHED) if turns_pair(stage) is not None]


def pair_turned(pair):
    return T_AT[PAIR_STAGE[pair] + 1]


def tile_used(i):
    _, l, b, buf = SCHED[i]
    if buf == "b":
        return max(j for j, s in enumerate(SCHED)
                   if j > i and (s[:2] == ("fc1" if l == 0 else "mlp1", b)))
    first = min(j for j, s in enumerate(SCHED) if j > i and s[0] in ("qkv", "proj"))
    return max(j for j, s in enumerate(SCHED) if s[:3] == SCHED[first][:3])


BACK_STAGE = [i for i, stage in enumerate(SCHED) if finishes(stage)[1] == 2]


def turned_back(gn):
    return S_AT[BACK_STAGE[gn] + 1]


def scores_ended(n):
    n0, b = n - n % B, n % B
    return T_AT[WHERE[("slot", n0, HG * (b + 1) - 1, NT - 1)]] + G


def hidden_parts(e):
    lo, parts = (e % E2) * HID, []
    while lo < (e % E2 + 1) * HID:
        hi = min((lo // P + 1) * P, (e % E2 + 1) * HID)
        parts.append((lo // P, lo % P, lo % P + hi - lo))
        lo = hi
    return parts


def added_before(i):
    same = [j for j in range(i) if SCHED[j][0] == "fc2" and SCHED[j][1] == SCHED[i][1] and
            SCHED[j][4] < SCHED[i][5] and SCHED[i][4] < SCHED[j][5]]
    return same[-1] + 1 if same else i


def turned_at(i):
    kind, b = SCHED[i][0], SCHED[i][2 if SCHED[i][0] in ("qkv", "proj") else 1]
    buf = "a" if kind in ("qkv", "proj") else "b"
    return T_AT[max(j for j in range(i) if SCHED[j][0] == "turn" and SCHED[j][2:] == (b, buf)) + 1]


def hidden_made(i, c):
    for j in range(i - 1, -1, -1):
        if SCHED[j][0] in ("fc1", "mlp1") and SCHED[j][3] <= c < SCHED[j][4]:
            return T_AT[j] + c - SCHED[j][3] + 1


def build(nc, t, out):
    ctx = ExitStack()
    with ctx:
        def sb(name, shape, dt=F32):
            return ctx.enter_context(nc.sbuf_tensor(name, shape, dt))

        def sem(name):
            return ctx.enter_context(nc.semaphore(name))

        banks = [ctx.enter_context(nc.psum_tensor(f"bank{i}", [P, 512], F32)) for i in range(8)]
        S_BANKS, T_BANKS, O_BANKS = banks[0:3], banks[3:6], banks[6:8]
        NS, NTB = len(S_BANKS), len(T_BANKS)

        qk_dram = nc.dram_tensor("qk_parts", (B * L, 2, PARTS, HD * NH, N), BF16, kind="Internal").ap()
        mod_dram = nc.dram_tensor("modulation", (L, 3, B, 2, C), F32, kind="Internal").ap()

        ident = sb("ident", [P, P])
        identb = sb("identb", [P, P], BF16)
        ones = sb("ones", [P, P])
        mask1 = sb("mask1", [P, 1])
        mask2 = sb("mask2", [P, 1])
        before = sb("before", [P, E, E])
        wqkv = [sb(f"wqkv{l}", [P, 3 * C]) for l in range(L)]
        wqk = [sb(f"wqk{l}", [P, 2 * C]) for l in range(L)]
        wqk_stk = [sb(f"wqk_stk{l}", [ROWS, 2 * C], BF16) for l in range(L)]
        wproj = [sb(f"wproj{l}", [P, C]) for l in range(L)]
        wgate = sb("wgate", [P, E])
        w1 = sb("w1", [P, E * HID])
        w2 = sb("w2", [P, CH * C])
        wfc1 = sb("wfc1", [P, HID])
        wfc2 = sb("wfc2", [P, CH1, C])
        wstk = sb("wstk", [ROWS, WN], BF16)
        b2bc = sb("b2bc", [P, E, C])
        bfc2 = sb("bfc2", [P, C])
        wada = [w1[:, l * 6 * C:(l + 1) * 6 * C] for l in range(L)]
        wadar = [w2[0:CR + 1, l * 6 * C:(l + 1) * 6 * C] for l in range(L)]
        cT = sb("cT", [P, B])
        cTr = sb("cTr", [CR, B])
        ex = sb("ex", [P, B])
        exr = sb("exr", [CR, B])
        siluB = sb("siluB", [P, B, P])
        siluBr = sb("siluBr", [CR + 1, B, P])
        mod = [sb(f"mod{l}", [P, B, 6, C]) for l in range(L)]
        x = sb("x", [P, B, NT, C])
        hN = sb("hN", [P, NT, C])
        stN = sb("stN", [P, NT, 100], BF16)
        rest = sb("rest", [P, NT, CR])
        oN = [sb(f"oN{b}", [P, NT, C]) for b in range(B)]
        hT = {"a": [sb("hTa", [P, N])] * B, "b": [sb(f"hTb{b}", [P, N]) for b in range(B)]}
        hS = {"a": [sb("hSa", [ROWS, N], BF16)] * B, "b": [sb(f"hSb{b}", [ROWS, N], BF16) for b in range(B)]}
        Qs = [sb(f"Qs{b}", [P, NH, N], BF16) for b in range(B)]
        Ks = [sb(f"Ks{b}", [P, NH, N], BF16) for b in range(B)]
        Va = [sb(f"Va{b}", [P, NT, NH, OW]) for b in range(B)]
        prob = sb("prob", [P, 2 * G * N])
        probs = prob[:, :].rearrange("p (k g n) -> p k g n", k=2, g=G)
        oT = sb("oT", [P, 2, N])
        nmax = sb("nmax", [P, 2, 2 * NT])
        mpart = sb("mpart", [P, 2, MPARTS, 2 * NT], BF16)
        mT = sb("mT", [MPARTS * 2 * NT, 2, P], BF16)
        rec = sb("rec", [P, NT, G])
        big = sb("big", [P, CHH * N])
        hmid = big[:, :].rearrange("p (c n) -> p c n", n=N)
        wraw = big[0:ROWS, 0:WN]
        qkf, qkp = [], []
        for place in (prob, prob, prob, big):
            qkf.append(place[:, 0:3 * N].rearrange("p (c n) -> p c n", c=3))
            qkp.append(place[:, 3 * N:3 * N + 9 * N // 2].bitcast(BF16)
                       .rearrange("p (c i n) -> p c i n", c=3, i=PARTS))
        stats = sb("stats", [P, B, NT, 6])
        mv = sb("mv", [P, B, NT, 2])
        var = sb("var", [P, B, NT])
        rs = sb("rs", [P, B, NT])
        nw = sb("nw", [P, B, 2, NT])
        lg = sb("lg", [P, NT, E])
        cmp = sb("cmp", [P, 2, NT, E, E])
        rank = sb("rank", [P, NT, E])
        gmax = sb("gmax", [P, NT])
        gex = sb("gex", [P, NT, E])
        gsum = sb("gsum", [P, NT])
        cw = [sb(f"cw{b}", [P, NT, E]) for b in range(B)]
        y = sb("y", [P, NT, C])
        attn = sb("attn", [P, NT, C])
        mod_row = {(l, part): place[0:B, 2 * half:2 * half + 2, :]
                   for l, part, place, half in ((0, 1, y, 0), (0, 2, y, 1), (1, 0, attn, 0), (1, 1, attn, 1),
                                                (1, 2, oN[1], 0))}

        ld_x = [sem(f"ld_x{b}") for b in range(B)]
        ld_c = sem("ld_c")
        ld_ada = [sem(f"ld_ada{l}") for l in range(L)]
        ld_qkv = sem("ld_qkv")
        ld_raw = [sem("ld_raw0"), sem("ld_raw1")]
        ld_w = [sem(f"ld_w{l}") for l in range(L)]
        c_ready = sem("c_ready")
        buf_ready = sem("buf_ready")
        v_ready = [sem(f"v_ready{b}") for b in range(B)]
        s_full, s_free = sem("s_full"), sem("s_free")
        t_full, t_free = sem("t_full"), sem("t_free")
        silu_exp = sem("silu_exp")
        silu_done = sem("silu_done")
        mod_out = sem("mod_out")
        mod_in = [[sem(f"mod_in{l}{part}") for part in range(3)] for l in range(L)]
        w_split = sem("w_split")
        w_ready = sem("w_ready")
        pool_step = sem("pool_step")
        main_ready = sem("main_ready")
        nat_ready = sem("nat_ready")
        qk_split = sem("qk_split")
        qk_out = [sem(f"qk_out{n}") for n in range(B * L)]
        qk_in = [[sem(f"qk_in{n}_{i}") for i in range(len(PIECES[n % B]))] for n in range(B * L)]
        m_first = sem("m_first")
        m_split = sem("m_split")
        m_in = [sem(f"m_in{i}") for i in range(4)]
        p_used = sem("p_used")
        o_copied = sem("o_copied")
        x_ready = sem("x_ready")
        logit_ready = sem("logit_ready")
        gate_exp = sem("gate_exp")
        cw_ready = sem("cw_ready")
        dve_step = sem("dve_step")
        stored = sem("stored")

        block = ctx.enter_context(nc.Block())

        @block.sync
        def _(sp):
            def row(v):
                return v.rearrange("(a n) -> a n", a=1)

            names = (("L0_cond_w_adaln", "L0_cond_b_adaln"), ("L1_cond_w_ada", "L1_cond_b_ada"))
            for b in range(B):
                sp.dma_start(x[:, b], t["x"][b].rearrange("(t p) c -> p t c", p=P)).then_inc(ld_x[b], 16)
            for l, (w, bias) in enumerate(names):
                sp.dma_start(wada[l], t[w][0:P]).then_inc(ld_ada[l], 16)
                sp.dma_start(wadar[l][0:CR], t[w][P:C]).then_inc(ld_ada[l], 16)
                sp.dma_start(wadar[l][CR:CR + 1], row(t[bias])).then_inc(ld_ada[l], 16)
                if l == 0:
                    sp.dma_start(wqkv[0][:, :], t["L0_cond_w_qkv"][0:P]).then_inc(ld_qkv, 16)

            w2f = t["L0_cond_w2"].rearrange("e h c -> (e h) c").rearrange("(k p) c -> p k c", p=P)
            full = HID // P
            late = [(mod_in[l][part], mod[l][:, :, 2 * part:2 * part + 2, :], mod_dram[l, part].partition_broadcast(P))
                    for l, part in ((0, 1), (0, 2))]
            late += [(ld_w[0], wproj[0][:, :], t["L0_cond_w_proj"][0:P]),
                     (ld_w[0], wgate[:, :], t["L0_cond_w_gate"][0:P])]
            late += [(ld_w[0], w1[:, e * HID:(e + 1) * HID], t["L0_cond_w1"][e, 0:P, :]) for e in range(E)]
            for k in range(0, CH, CH // 3):
                late.append((ld_w[0], w2[:, k * C:(k + CH // 3) * C].rearrange("p (k c) -> p k c", c=C),
                             w2f[:, k:k + CH // 3, :]))
            late += [(ld_w[0], b2bc[:, :, :], t["L0_cond_b2"].partition_broadcast(P)),
                     (ld_w[1], wqkv[1][:, :], t["L1_cond_w_qkv"][0:P]),
                     (ld_w[1], wproj[1][:, :], t["L1_cond_w_proj"][0:P]),
                     (ld_w[1], wfc1[:, :], t["L1_cond_w_fc1"][0:P]),
                     (ld_w[1], wfc2[:, 0:full, :], t["L1_cond_w_fc2"][0:full * P].rearrange("(k p) c -> p k c", p=P)),
                     (ld_w[1], wfc2[0:HID - full * P, full, :], t["L1_cond_w_fc2"][full * P:HID]),
                     (ld_w[1], bfc2[:, :], t["L1_cond_b_fc2"].partition_broadcast(P))]
            late += [(mod_in[1][part], mod[1][:, :, 2 * part:2 * part + 2, :], mod_dram[1, part].partition_broadcast(P))
                     for part in range(3)]
            assert len(late) == LATE0 + LATE1 + 3 * L - 1

            for i, stage in enumerate(SCHED):
                if stage[0] == "qkv":
                    _, l, b, first, last = stage
                    n = B * l + b
                    parts = qk_dram[n]
                    main = (HD - 1) * NH
                    for c, w, r, rows, lo in ((0, 0, 0, main, 0), (1, 1, 0, main, 0),
                                              (2, 0, 0, NH, main), (2, 1, NH, NH, main)):
                        if not first <= c < last:
                            continue
                        sp.wait_ge(qk_split, 3 * n + c + 1)
                        sp.dma_start(parts[w, :, lo:lo + rows, :].rearrange("i r n -> r i n"),
                                     qkp[n][r:r + rows, c, :, :]).then_inc(qk_out[n], 16)
                for n, piece in pieces_after(stage):
                    b, parts = n % B, qk_dram[n]
                    sp.wait_ge(qk_out[n], 4 * 16)
                    if n < B:
                        sp.wait_ge(buf_ready, n + 1)
                    else:
                        sp.wait_ge(t_full, scores_ended(n - B))
                    lo, hi = PIECES[b][piece]
                    width, cols, done = (hi - lo) * N, slice(lo * N, hi * N), qk_in[n][piece]
                    src = parts[1].rearrange("j (d h) n -> (j d) (h n)", h=NH)[:, cols]
                    sp.dma_start(Ks[b][0:PAIRS, lo:hi, :],
                                 src.unsqueeze(0).to_broadcast([PARTS, PARTS * HD, width])).then_inc(done, 16)
                    for i_ in range(PARTS):
                        r = HD * PARTS * i_
                        src = parts[0, i_].rearrange("(d h) n -> d (h n)", h=NH)[:, cols]
                        sp.dma_start(Qs[b][r:r + HD * PARTS, lo:hi, :],
                                     src.unsqueeze(0).to_broadcast([PARTS, HD, width])).then_inc(done, 16)
                if stage[0] == "ada" and stage[1:] != (0, 0):
                    _, l, part = stage
                    sp.wait_ge(t_free, T_AT[i + 1])
                    sp.dma_start(mod_dram[l, part], mod_row[l, part]).then_inc(mod_out, 16)
                if stage == ("max", 0, UNIT_LEAD - 1):
                    sp.wait_ge(mod_out, 16 * (3 * L - 1))
                if stage[0] == "slot" and late:
                    done, place, source = late.pop(0)
                    sp.dma_start(place, source).then_inc(done, 16)
                pair = turns_pair(stage)
                if pair is not None:
                    n, h = 2 * pair // NH, 2 * pair % NH
                    sp.wait_ge(t_free, T_AT[i + 1])
                    if n < B:
                        sp.wait_ge(buf_ready, n + 1)
                    else:
                        sp.wait_ge(t_full, scores_ended(n - B))
                    sp.dma_start(Qs[n % B][MROW:SROWS, h:h + 2, :], mT[:, pair % 2, :]).then_inc(m_in[pair % 4], 16)

        @block.gpsimd
        def _(pool):
            G_ = nc.gpsimd
            sources = {"qkv0": ("L0_cond_w_qkv", "L0_cond_b_qkv"), "proj0": ("L0_cond_w_proj", "L0_cond_b_proj"),
                       "gate": ("L0_cond_w_gate", None), "w1": ("L0_cond_w1", "L0_cond_b1"),
                       "qkv1": ("L1_cond_w_qkv", "L1_cond_b_qkv"), "proj1": ("L1_cond_w_proj", "L1_cond_b_proj"),
                       "fc1": ("L1_cond_w_fc1", "L1_cond_b_fc1")}

            def load_raw(name):
                done = ld_raw[name != "qkv0"]
                w, bias = sources[name]
                a, n = WCOLS[name]
                for rows in STACK.values():
                    lo, k = rows[0][0], len(rows)
                    if name == "w1":
                        for e in range(E):
                            src = t[w][e, P:C, :].unsqueeze(0).to_broadcast([k, CR, HID])
                            pool.dma_start(wraw[lo:lo + k * CR, a + e * HID:a + (e + 1) * HID], src).then_inc(done, 16)
                    else:
                        src = t[w][P:C, :].unsqueeze(0).to_broadcast([k, CR, n])
                        pool.dma_start(wraw[lo:lo + k * CR, a:a + n], src).then_inc(done, 16)
                for r in BIAS_ROWS:
                    if bias is not None:
                        src = t[bias].rearrange("e h -> (e h)") if name == "w1" else t[bias]
                        pool.dma_start(wraw[r:r + 1, a:a + n], src.rearrange("(o n) -> o n", o=1)).then_inc(done, 16)

            step = [0]

            def link(ins):
                step[0] += 1
                ins.then_inc(pool_step, 1)
                pool.wait_ge(pool_step, step[0])

            def split_weights(a, n):
                raw, stk = wraw[:, a:a + n], wstk[:, a:a + n]
                link(G_.tensor_copy(stk, raw))
                link(G_.tensor_scalar(stk, stk, mask1[0:ROWS, 0:1], 0.0, ALU.mult, ALU.add))
                link(G_.tensor_tensor(raw, raw, stk, ALU.add))
                link(G_.tensor_copy(stk, raw))
                link(G_.tensor_scalar(stk, stk, mask2[0:ROWS, 0:1], 0.0, ALU.mult, ALU.add))
                return G_.tensor_tensor(stk, raw, stk, ALU.add)

            load_raw("qkv0")
            G_.memset(mask1[:, :], -1.0)
            G_.memset(mask2[:, :], -1.0)
            G_.memset(ident[:, :], 0.0)
            G_.memset(identb[:, :], 0.0)
            G_.memset(before[:, :, :], 1.0)
            link(G_.memset(wraw[:, WCOLS["gate"][0]:WCOLS["gate"][0] + E], 0.0))
            for m, first in ((mask1, MASK1), (mask2, MASK2)):
                G_.affine_select(out=m[:, :], in_=m[:, :], compare_op=ALU.is_ge, fill=0.0, base=-first,
                                 pattern=[[0, 1]], channel_multiplier=1)
            for m in (ident, identb):
                G_.affine_select(out=m[:, :], in_=m[:, :], compare_op=ALU.not_equal, fill=1.0, base=0,
                                 pattern=[[-1, P]], channel_multiplier=1)
            G_.affine_select(out=before[:, :, :], in_=before[:, :, :], compare_op=ALU.is_gt, fill=0.0, base=0,
                             pattern=[[1, E], [-1, E]], channel_multiplier=0).then_inc(c_ready, 1)
            pool.wait_ge(c_ready, 1)
            pool.wait_ge(ld_raw[0], 16 * 6)
            split_weights(*WCOLS["qkv0"]).then_inc(w_split, 1)
            pool.wait_ge(w_split, 1)
            pair_of_ones = 0x3F803F80
            for b in range(B):
                G_.memset(Qs[b][64:96, :, :].bitcast(I32), 0)
                link(G_.memset(Ks[b][64:96, :, :].bitcast(I32), 0))
                G_.memset(Ks[b][96:SROWS, :, :].bitcast(I32), pair_of_ones).then_inc(buf_ready, 1)
                pool.wait_ge(buf_ready, b + 1)
                if b == 0:
                    link(G_.memset(Va[1][:, :, :, :], 0.0))
                    G_.memset(Va[1][:, :, :, HD:HD + 1], 1.0).then_inc(v_ready[1], 1)
                    pool.wait_ge(v_ready[1], 1)
            for name in sources:
                if name != "qkv0":
                    load_raw(name)
            pool.wait_ge(ld_raw[1], 16 * (5 * 3 + 3 * E + 5 * 3))
            for k, (name, last) in enumerate((("proj0", "gate"), ("w1", "w1"), ("qkv1", "fc1"))):
                a = WCOLS[name][0]
                split_weights(a, sum(WCOLS[last]) - a).then_inc(w_split, 1)

        @block.vector
        def _(dve):
            V = nc.vector
            step = [0]

            def signal(ins):
                step[0] += 1
                ins.then_inc(dve_step, 1)
                return step[0]

            def link(ins):
                dve.wait_ge(dve_step, signal(ins))

            def take(at):
                dve.wait_ge(s_full, at + 1)
                return S_BANKS[at % NS]

            turn_stages = [i for i, stage in enumerate(SCHED) if stage[0] == "turn"]
            prepared = [0]

            def natural_free():
                if prepared[0]:
                    dve.wait_ge(t_full, T_AT[turn_stages[prepared[0] - 1] + 1])
                prepared[0] += 1

            def split_stack(src):
                col = {part: [r for rows in STACK.values() for r, q in rows if q == part] for part in range(PARTS)}
                at = {part: [stN[:, :, r:r + CR] for r in rows] for part, rows in col.items()}
                done = signal(V.tensor_copy(at[0][0], src))
                yield
                dve.wait_ge(dve_step, done)
                V.tensor_copy(at[0][1], at[0][0]).then_inc(main_ready, 1)
                V.tensor_copy(at[0][2], at[0][0])
                done = signal(V.tensor_tensor(rest[:, :, :], src, at[0][0], ALU.subtract))
                yield
                dve.wait_ge(dve_step, done)
                done = signal(V.tensor_copy(at[1][0], rest[:, :, :]))
                yield
                dve.wait_ge(dve_step, done)
                done = signal(V.tensor_copy(at[1][1], at[1][0]))
                yield
                dve.wait_ge(dve_step, done)
                V.tensor_tensor(at[2][0], rest[:, :, :], at[1][0], ALU.subtract).then_inc(nat_ready, 1)

            def heads_innermost(l):
                a = WCOLS[f"qkv{l}"][0]
                for src, dst in ((wqkv[l][:, :], wqk[l][:, :]), (wstk[:, a:a + 3 * C], wqk_stk[l][:, :])):
                    for w in range(2):
                        ins = V.tensor_copy(dst[:, w * P:(w + 1) * P].rearrange("p (d h) -> p d h", h=NH),
                                      src[:, w * C:(w + 1) * C].rearrange("p (h d) -> p d h", d=HD)[:, 0:HD - 1, :])
                    ins = V.tensor_copy(dst[:, 2 * P:2 * C], src[:, HD - 1:2 * C:HD])
                ins.then_inc(w_ready, 1)

            def norm(bs, l, b, shift, scale, amid=True):
                for c in range(B)[bs]:
                    for k in range(NT):
                        ins = V.bn_stats(stats[:, c, k, :], x[:, c, k, :])
                done = signal(ins)
                yield
                dve.wait_ge(dve_step, done)
                for c in range(B)[bs]:
                    for k in range(NT):
                        ins = V.bn_aggr(mv[:, c, k, :], stats[:, c, k, :])
                done = signal(ins)
                yield
                dve.wait_ge(dve_step, done)
                natural_free()

                def centre(tiles):
                    for k in tiles:
                        ins = V.scalar_tensor_tensor(hN[:, k, :], x[:, b, k, :], mv[:, b, k, 0:1],
                                                     mod[l][:, b, scale, :], ALU.subtract, ALU.mult)
                    return ins

                done = signal(V.tensor_scalar(var[:, bs, :], mv[:, bs, :, 1], EPS, None, ALU.add))
                yield
                dve.wait_ge(dve_step, done)
                r, bits = rs[:, bs, :], rs[:, bs, :].bitcast(I32)
                done = signal(V.tensor_single_scalar(bits, var[:, bs, :].bitcast(I32), 1, ALU.arith_shift_right))
                yield
                dve.wait_ge(dve_step, done)
                done = signal(V.tensor_scalar(bits, bits, -1.0, float(0x5F3759DF), ALU.mult, ALU.add))
                yield
                dve.wait_ge(dve_step, done)
                for newton in range(3):
                    if amid:
                        centre([newton])
                    done = signal(V.tensor_tensor(nw[:, bs, 0, :], r, r, ALU.mult))
                    yield
                    dve.wait_ge(dve_step, done)
                    if amid and newton == 1:
                        centre([3])
                    done = signal(V.scalar_tensor_tensor(nw[:, bs, 1, :], nw[:, bs, 0, :], -0.5, var[:, bs, :],
                                                         ALU.mult, ALU.mult))
                    yield
                    dve.wait_ge(dve_step, done)
                    done = signal(V.scalar_tensor_tensor(r, nw[:, bs, 1, :], 1.5, r, ALU.add, ALU.mult))
                    yield
                    dve.wait_ge(dve_step, done)
                if not amid:
                    dve.wait_ge(t_free, T_AT[WHERE[("ada", 0, 0)] + 1])
                    done = signal(centre(range(NT)))
                    yield
                    dve.wait_ge(dve_step, done)
                yield from norm_end(l, b, shift)

            def norm_end(l, b, shift):
                for k in range(NT):
                    ins = V.scalar_tensor_tensor(hN[:, k, :], hN[:, k, :], rs[:, b, k:k + 1], mod[l][:, b, shift, :],
                                                 ALU.mult, ALU.add)
                done = signal(ins)
                yield
                dve.wait_ge(dve_step, done)
                yield from split_stack(hN[:, :, P:C])

            def norm_again(l, b, shift, scale):
                natural_free()
                for k in range(NT):
                    ins = V.scalar_tensor_tensor(hN[:, k, :], x[:, b, k, :], mv[:, b, k, 0:1], mod[l][:, b, scale, :],
                                                 ALU.subtract, ALU.mult)
                done = signal(ins)
                yield
                dve.wait_ge(dve_step, done)
                yield from norm_end(l, b, shift)

            beside = []

            def advance():
                while beside:
                    if next(beside[0], "ended") != "ended":
                        return
                    beside.pop(0)

            def finish():
                while beside:
                    advance()

            def split_max_first(pair, s_at):
                if pair >= 2:
                    dve.wait_ge(t_full, pair_turned(pair - 2))
                dve.wait_ge(s_free, s_at)
                V.tensor_copy(mpart[:, pair % 2, 0, :], nmax[:, pair % 2, :]).then_inc(m_first, 1)

            def split_max_second(pair):
                dve.wait_ge(m_first, pair + 1)
                V.tensor_tensor(mpart[:, pair % 2, 1, :], nmax[:, pair % 2, :], mpart[:, pair % 2, 0, :],
                                ALU.subtract).then_inc(m_split, 1)

            def gate_rows(l, b, gate, tiles):
                return mod[l][:, b, gate, :].unsqueeze(1).to_broadcast([P, tiles, C])

            def split_chunk(n, c, copied):
                rows = (P, P, 2 * NH)[c]
                f, q = qkf[n][0:rows, c, :], qkp[n]
                dve.wait_ge(t_free, copied)
                done = signal(V.tensor_tensor(f, f, q[0:rows, c, 0, :], ALU.subtract))
                yield
                dve.wait_ge(dve_step, done)
                done = signal(V.tensor_copy(q[0:rows, c, 1, :], f))
                yield
                dve.wait_ge(dve_step, done)
                V.tensor_tensor(q[0:rows, c, 2, :], f, q[0:rows, c, 1, :], ALU.subtract).then_inc(qk_split, 1)

            def add_experts(b):
                done = signal(V.tensor_tensor(y[:, :, :], y[:, :, :], gate_rows(0, b, 5, NT), ALU.mult))
                yield
                dve.wait_ge(dve_step, done)
                done = signal(V.tensor_tensor(x[:, b], x[:, b], y[:, :, :], ALU.add))
                yield
                dve.wait_ge(dve_step, done)

            def add_mlp(b, read):
                dve.wait_ge(s_free, read)
                done = signal(V.tensor_tensor(y[:, :, :], y[:, :, :], gate_rows(1, b, 5, NT), ALU.mult))
                yield
                dve.wait_ge(dve_step, done)
                V.tensor_tensor(x[:, b], x[:, b], y[:, :, :], ALU.add).then_inc(x_ready, 1)

            for r in BIAS_ROWS:
                V.memset(stN[:, :, r:r + 1], 1.0)
            V.memset(ones[:, :], 1.0)
            V.memset(siluBr[:, :, :], 1.0)
            link(V.memset(Va[0][:, :, :, :], 0.0))
            V.memset(Va[0][:, :, :, HD:HD + 1], 1.0).then_inc(v_ready[0], 1)

            for i, stage in enumerate(SCHED):
                kind, s_at = stage[0], S_AT[i]
                if kind == "ada":
                    if stage[1:] == (0, 0):
                        dve.wait_ge(silu_exp, 2)
                        V.tensor_scalar(ex[:, :], ex[:, :], 1.0, None, ALU.add)
                        link(V.tensor_scalar(exr[:, :], exr[:, :], 1.0, None, ALU.add))
                        V.reciprocal(ex[:, :], ex[:, :])
                        link(V.reciprocal(exr[:, :], exr[:, :]))
                        V.tensor_tensor(cT[:, :], cT[:, :], ex[:, :], ALU.mult)
                        link(V.tensor_tensor(cTr[:, :], cTr[:, :], exr[:, :], ALU.mult))
                        for b in range(B):
                            V.tensor_scalar(siluB[:, b, :], ones[:, :], cT[:, b:b + 1], None, ALU.mult)
                            ins = V.tensor_scalar(siluBr[0:CR, b, :], ones[0:CR, :], cTr[:, b:b + 1], None, ALU.mult)
                        ins.then_inc(silu_done, 1)
                elif kind == "ln":
                    _, l, which = stage
                    b = which % B
                    for part in range(3):
                        if l or which >= B and part:
                            dve.wait_ge(mod_in[l][part], 16)
                    at = 3 * (which // B)
                    if stage == ("ln", 0, 0):
                        for c in range(B):
                            dve.wait_ge(ld_x[c], 16)
                        beside.append(norm(slice(0, B), l, b, at, at + 1, amid=False))
                    elif stage == ("ln", 0, 1):
                        beside.append(norm_again(l, b, at, at + 1))
                    else:
                        beside.append(norm(slice(b, b + 1), l, b, at, at + 1))
                elif kind == "turn":
                    finish()
                    if prepared[0] == 1:
                        dve.wait_ge(ld_qkv, 16)
                        dve.wait_ge(w_split, 1)
                        heads_innermost(0)
                elif kind == "qkv":
                    _, l, b, first, last = stage
                    n = B * l + b
                    chunks = [c for c in range(3) if first <= c < last]
                    if n == B * L - 1:
                        for c in chunks:
                            beside.append(split_chunk(n, c, T_AT[i] + c - first + 1))
                        continue
                    finish()
                    chunks = [split_chunk(n, c, T_AT[i] + c + 1) for c in chunks]
                    for part in range(PARTS):
                        for chunk in chunks:
                            next(chunk, None)
                elif kind == "osplit":
                    _, l, b = stage
                    finish()
                    natural_free()
                    beside.append(split_stack(oN[b][:, :, P:C]))
                    finish()
                elif kind == "proj":
                    _, l, b = stage
                    dve.wait_ge(mod_in[l][1], 16)
                    for k in range(NT // 2):
                        bank = take(s_at + k)
                        V.tensor_tensor(attn[:, 2 * k:2 * k + 2, :],
                                        bank[:, 0:2 * C].rearrange("p (t c) -> p t c", t=2),
                                        gate_rows(l, b, 2, 2), ALU.mult).then_inc(s_free, 1)
                    dve.wait_ge(s_free, s_at + NT // 2)
                    link(V.tensor_tensor(x[:, b], x[:, b], attn[:, :, :], ALU.add))
                elif kind == "gate":
                    b = stage[1]
                    bank = take(s_at)
                    V.tensor_copy(lg[:, :, :], bank[:, 0:NT * E].rearrange("p (t e) -> p t e", e=E)).then_inc(s_free, 1)
                    dve.wait_ge(s_free, s_at + 1)
                    me = lg[:, :, :].unsqueeze(3).to_broadcast([P, NT, E, E])
                    other = lg[:, :, :].unsqueeze(2).to_broadcast([P, NT, E, E])
                    V.tensor_tensor(cmp[:, 0], other, me, ALU.is_gt)
                    V.tensor_tensor(cmp[:, 1], other, me, ALU.is_equal)
                    link(V.tensor_reduce(gmax[:, :], lg[:, :, :], AX.X, ALU.max))
                    V.tensor_tensor(lg[:, :, :], lg[:, :, :], gmax[:, :].unsqueeze(2).to_broadcast([P, NT, E]),
                                    ALU.subtract).then_inc(logit_ready, 1)
                    early = before[:, :, :].unsqueeze(1).to_broadcast([P, NT, E, E])
                    link(V.tensor_tensor(cmp[:, 1], cmp[:, 1], early, ALU.mult))
                    link(V.tensor_tensor(cmp[:, 0], cmp[:, 0], cmp[:, 1], ALU.add))
                    link(V.tensor_reduce(rank[:, :, :], cmp[:, 0], AX.X, ALU.add))
                    dve.wait_ge(gate_exp, b + 1)
                    link(V.scalar_tensor_tensor(gex[:, :, :], rank[:, :, :], 2.0, gex[:, :, :], ALU.is_lt, ALU.mult))
                    link(V.tensor_reduce(gsum[:, :], gex[:, :, :], AX.X, ALU.add))
                    link(V.reciprocal(gsum[:, :], gsum[:, :]))
                    V.tensor_tensor(cw[b][:, :, :], gex[:, :, :], gsum[:, :].unsqueeze(2).to_broadcast([P, NT, E]),
                                    ALU.mult).then_inc(cw_ready, 1)
                elif kind in ("fc1", "mlp1"):
                    finish()
                    if stage == ("fc1", 0, 1, 0, CHH):
                        dve.wait_ge(ld_w[1], 16 * LATE1)
                        dve.wait_ge(w_split, 4)
                        heads_innermost(1)
                elif kind == "fc2":
                    _, b, half, e2, lo, hi = stage
                    if half == 0 and e2 == 0 and lo == 0:
                        dve.wait_ge(cw_ready, b + 1)
                        dve.wait_ge(ld_w[0], 16 * LATE0)
                        finish()
                        for e in range(E):
                            for k in range(NT):
                                if e == 0:
                                    ins = V.tensor_scalar(y[:, k, :], b2bc[:, 0, :], cw[b][:, k, 0:1], None, ALU.mult)
                                else:
                                    ins = V.scalar_tensor_tensor(y[:, k, :], b2bc[:, e, :], cw[b][:, k, e:e + 1],
                                                                 y[:, k, :], ALU.mult, ALU.add)
                            link(ins)
                    e = E2 * half + e2
                    dve.wait_ge(s_free, S_AT[added_before(i)])
                    for k in range(lo, hi):
                        bank = take(s_at + k - lo)
                        V.scalar_tensor_tensor(y[:, k, :], bank[:, 0:C], cw[b][:, k, e:e + 1], y[:, k, :],
                                               ALU.mult, ALU.add).then_inc(s_free, 1)
                        for _ in range(3):
                            advance()
                    dve.wait_ge(s_free, S_AT[i + 1])
                    if half and e2 and hi == NT:
                        beside.append(add_experts(b))
                elif kind == "mlp2":
                    b = stage[1]
                    if b:
                        finish()
                        dve.wait_ge(x_ready, b)
                    for k in range(NT):
                        bank = take(s_at + k)
                        V.tensor_tensor(y[:, k, :], bank[:, 0:C], bfc2[:, :], ALU.add).then_inc(s_free, 1)
                        if b < B - 1:
                            for _ in range(4):
                                advance()
                        else:
                            dve.wait_ge(s_free, s_at + k + 1)
                            link(V.tensor_tensor(y[:, k, :], y[:, k, :], mod[1][:, b, 5, :], ALU.mult))
                            ins = V.tensor_tensor(x[:, b, k, :], x[:, b, k, :], y[:, k, :], ALU.add)
                            if k % 2:
                                ins.then_inc(x_ready, 1)
                    if b < B - 1:
                        beside.append(add_mlp(b, S_AT[i + 1]))
                u = unit_of(stage)
                if u is not None:
                    pair, odd = (NH * stage[1] + u) // 2, u % 2
                    half = pair % 2
                    for k in range(*tiles_of(stage)):
                        bank = take(s_at + k - tiles_of(stage)[0])
                        V.tensor_reduce(nmax[:, half, odd * NT + k:odd * NT + k + 1], bank[:, :], AX.X, ALU.max,
                                        negate=True).then_inc(s_free, 1)
                        if k == 0 and not odd and u:
                            split_max_first(pair - 1, s_at)
                        elif k == 1 and not odd and u:
                            split_max_second(pair - 1)
                        else:
                            advance()
                            if stage[1] and u < B * NH // 2:
                                advance()
                if turns_pair(stage) is not None and u is None:
                    split_max_first(turns_pair(stage), s_at)
                    split_max_second(turns_pair(stage))
                g, k = finishes(stage)
                if k == 1 and kind == "tail":
                    gn = HG * stage[1] + g
                    dve.wait_ge(p_used, NT * (gn + 1))
                    dve.wait_ge(s_full, turned_back(gn - 2))
                    V.tensor_copy(oT[:, gn % 2, :], O_BANKS[gn % 2][:, :]).then_inc(o_copied, 1)
                if k == 2:
                    b, hg = g // HG, g % HG
                    at = S_AT[i + 1] - 1
                    o = take(at)[:, :].rearrange("p (t g w) -> p t g w", t=NT, g=G)
                    link(V.reciprocal(rec[:, :, :], o[:, :, :, HD]))
                    dst = oN[b][:, :, hg * G * HD:(hg + 1) * G * HD].rearrange("p t (g d) -> p t g d", d=HD)
                    V.tensor_tensor(dst, o[:, :, :, 0:HD], rec[:, :, :].unsqueeze(3).to_broadcast([P, NT, G, HD]),
                                    ALU.mult).then_inc(s_free, 1)
                    dve.wait_ge(s_free, at + 1)

        @block.scalar
        def _(act):
            A = nc.scalar
            last_use = {}

            def take(at):
                act.wait_ge(t_full, at + 1)
                return T_BANKS[at % NTB]

            act.dma_start(cT[:, :], t["cond_1152"][:, 0:P].rearrange("b c -> c b"),
                          allow_slow_non_contiguous=True).then_inc(ld_c, 16)
            act.dma_start(cTr[:, :], t["cond_1152"][:, P:C].rearrange("b c -> c b"),
                          allow_slow_non_contiguous=True).then_inc(ld_c, 16)

            for i, stage in enumerate(SCHED):
                kind, t_at = stage[0], T_AT[i]
                if kind == "ada":
                    _, l, part = stage
                    if stage[1:] == (0, 0):
                        act.wait_ge(ld_c, 32)
                        A.activation(ex[:, :], cT[:, :], ACT.Exp, scale=-1.0).then_inc(silu_exp, 1)
                        A.activation(exr[:, :], cTr[:, :], ACT.Exp, scale=-1.0).then_inc(silu_exp, 1)
                    for j in range(B if stage[1:] == (0, 0) else 1):
                        bank = take(t_at + j)
                        for r in range(2):
                            bias = 1.0 if 2 * part + r in (1, 4) else 0.0
                            cols = slice(r * C, (r + 1) * C)
                            if stage[1:] == (0, 0):
                                ins = A.activation(mod[0][:, j, r, :], bank[:, cols], ACT.Copy, bias=bias)
                            else:
                                ins = A.activation(mod_row[l, part][:, r, :], bank[0:B, cols], ACT.Copy, bias=bias)
                        ins.then_inc(t_free, 1)
                elif kind == "turn":
                    _, l, b, buf = stage
                    key = buf if buf == "a" else (buf, b)
                    if key in last_use:
                        j = last_use[key]
                        if SCHED[j][0] == "proj":
                            act.wait_ge(s_full, S_AT[j + 1])
                        else:
                            act.wait_ge(t_full, T_AT[j + 1])
                    last_use[key] = tile_used(i)
                    bank = take(t_at)
                    A.activation(hT[buf][b][:, :], bank[:, :], ACT.Copy).then_inc(t_free, 1)
                    bank = take(t_at + 1)
                    A.activation(hS[buf][b][:, :], bank[0:ROWS, 0:N // 2].bitcast(BF16), ACT.Copy).then_inc(t_free, 1)
                elif kind == "qkv":
                    _, l, b, first, last = stage
                    n = B * l + b
                    if n and first == 0:
                        act.wait_ge(qk_out[n - 1], 4 * 16)
                    if n == B:
                        act.wait_ge(p_used, NT * B * HG)
                    if n == B + 1 and first == 0:
                        act.wait_ge(s_full, S_AT[WHERE[("fc2", 1, 1, 1, NT - 1, NT)] + 1])
                    for c in range(first, last):
                        bank = take(t_at + c - first)
                        if c < 3:
                            rows = (P, P, 2 * NH)[c]
                            A.activation(qkf[n][0:rows, c, :], bank[0:rows, :], ACT.Copy)
                            A.activation(qkp[n][0:rows, c, 0, :], bank[0:rows, :], ACT.Copy).then_inc(t_free, 1)
                            continue
                        if c == 3 and n < B:
                            act.wait_ge(v_ready[n], 1)
                        elif c == 3:
                            act.wait_ge(p_used, NT * HG * (n - 1))
                        k = c - 3
                        A.activation(Va[b][:, 2 * k:2 * k + 2, :, 0:HD],
                                     bank[:, 0:2 * C].rearrange("p (t h d) -> p t h d", t=2, d=HD),
                                     ACT.Copy).then_inc(t_free, 1)
                elif kind == "gate":
                    b = stage[1]
                    act.wait_ge(logit_ready, b + 1)
                    if b:
                        act.wait_ge(cw_ready, b)
                    A.activation(gex[:, :, :], lg[:, :, :], ACT.Exp).then_inc(gate_exp, 1)
                elif kind in ("fc1", "mlp1"):
                    lo, hi = stage[3:5]
                    prev = [j for j in range(i) if SCHED[j][0] in ("fc2", "mlp2")]
                    if prev and lo == 0:
                        act.wait_ge(s_full, S_AT[prev[-1] + 1])
                    if stage[:2] == ("mlp1", 0) and lo == 0:
                        act.wait_ge(qk_out[B * L - 1], 4 * 16)
                    if kind == "fc1" and stage[1:] == (0, 0, 0, CHH):
                        act.wait_ge(w_split, 4)
                    for c in range(lo, hi):
                        rows = P if kind == "fc1" else min(P, HID - c * P)
                        bank = take(t_at + c - lo)
                        A.activation(hmid[0:rows, c, :], bank[0:rows, :], ACT.Gelu_apprx_tanh).then_inc(t_free, 1)
                if kind == "slot":
                    _, n0, g, k = stage
                    done = NT * (HG * n0 + g) + k
                    if g == 0 and k == 0:
                        act.wait_ge(qk_out[1 if n0 == 0 else B], 4 * 16)
                    for j in range(G):
                        bank = take(t_at + j)
                        if done >= 2 and j == 0:
                            act.wait_ge(p_used, done - 1)
                        A.activation(probs[:, k % 2, j, :], bank[:, :], ACT.Exp, scale=SCALE).then_inc(t_free, 1)
                pair = turns_pair(stage)
                if pair is not None:
                    if pair >= 2:
                        act.wait_ge(m_in[(pair - 2) % 4], 16 * ((pair - 2) // 4 + 1))
                    bank = take(T_AT[i + 1] - 1)
                    A.activation(mT[:, pair % 2, :], bank[0:MPARTS * 2 * NT, 0:P // 2].bitcast(BF16), ACT.Copy)\
                        .then_inc(t_free, 1)
                g, k = finishes(stage)
                if k == 1 and kind == "slot":
                    gn = HG * stage[1] + g
                    act.wait_ge(p_used, NT * (gn + 1))
                    if gn >= 2:
                        act.wait_ge(s_full, turned_back(gn - 2))
                    A.activation(oT[:, gn % 2, :], O_BANKS[gn % 2][:, :], ACT.Copy).then_inc(o_copied, 1)
            for n, (b, tiles) in enumerate(((0, slice(0, NT)), (1, slice(0, NT // 2)), (1, slice(NT // 2, NT)))):
                act.wait_ge(x_ready, n + 1)
                act.dma_start(out[b].rearrange("(t p) c -> p t c", p=P)[:, tiles, :],
                              x[:, b, tiles, :]).then_inc(stored, 16)
            act.wait_ge(stored, 16 * 3)

        @block.tensor
        def _(pe):
            M = nc.tensor
            turns = [0]
            from_attention = set()

            def fill_s(at):
                if at >= NS:
                    pe.wait_ge(s_free, at - NS + 1)
                return S_BANKS[at % NS]

            def fill_t(at):
                if at >= NTB:
                    pe.wait_ge(t_free, at - NTB + 1)
                return T_BANKS[at % NTB]

            def stacked(name, lo, hi):
                a, _ = WCOLS[name]
                return wstk[:, a + lo:a + hi]

            def second(n0, g, k):
                gn = HG * n0 + g
                b, h0 = g // HG, G * (g % HG)
                if k == 0 and gn >= 2:
                    pe.wait_ge(o_copied, gn - 1)
                pe.wait_ge(t_free, T_AT[WHERE[("slot", n0, g, k)]] + G)
                for j in range(G):
                    ins = M.matmul(O_BANKS[gn % 2][OW * j:OW * (j + 1), :], Va[b][:, k, h0 + j, :],
                                   probs[:, k % 2, j, :], start=(k == 0), stop=(k == NT - 1), skip_group_check=True)
                ins.then_inc(p_used, 1)

            for i, stage in enumerate(SCHED):
                kind, s_at, t_at = stage[0], S_AT[i], T_AT[i]
                if kind == "ada":
                    _, l, part = stage
                    pe.wait_ge(silu_done, 1)
                    pe.wait_ge(ld_ada[l], 48)
                    cols = slice(2 * C * part, 2 * C * (part + 1))
                    outs = [(P, siluB[:, b, :], siluBr[:, b, :]) for b in range(B)]
                    if stage[1:] != (0, 0):
                        outs = [(B, siluB[:, :, 0], siluBr[:, :, 0])]
                    for j, (rows, main, others) in enumerate(outs):
                        bank = fill_t(t_at + j)
                        M.matmul(bank[0:rows, 0:2 * C], main, wada[l][:, cols], start=True, stop=False)
                        M.matmul(bank[0:rows, 0:2 * C], others, wadar[l][:, cols], start=False, stop=True)\
                            .then_inc(t_full, 1)
                elif kind == "turn":
                    _, l, b, buf = stage
                    turns[0] += 1
                    if turns[0] == 1:
                        pe.wait_ge(c_ready, 1)
                    pe.wait_ge(main_ready, turns[0])
                    src = oN[b] if (l, b, buf) in from_attention else hN
                    from_attention.add((l, b, "a"))
                    bank = fill_t(t_at)
                    for k in range(NT):
                        ins = M.transpose(bank[:, k * P:(k + 1) * P], src[:, k, 0:P], ident[:, :])
                    ins.then_inc(t_full, 1)
                    pe.wait_ge(nat_ready, turns[0])
                    view = fill_t(t_at + 1)[0:ROWS, 0:N // 2].bitcast(BF16)
                    for k in range(NT):
                        ins = M.transpose(view[:, k * P:(k + 1) * P], stN[:, k, 0:ROWS], identb[:, :])
                    ins.then_inc(t_full, 1)
                elif kind == "qkv":
                    _, l, b, first, last = stage
                    h, s = hT["a"][b], hS["a"][b]
                    turned = turned_at(i)
                    pe.wait_ge(t_free, turned - 1)
                    pe.wait_ge(w_ready, 1 + l)
                    pe.wait_ge(*((ld_qkv, 16) if l == 0 else (ld_w[1], 16 * LATE1)))
                    for c, lo, cols in ((0, 0, P), (1, P, P), (2, 2 * P, 2 * NH)):
                        if first <= c < last:
                            bank = fill_t(t_at + c - first)
                            M.matmul(bank[0:cols, :], wqk[l][:, lo:lo + cols], h[:, :], start=True, stop=False)
                            pe.wait_ge(t_free, turned)
                            M.matmul(bank[0:cols, :], wqk_stk[l][:, lo:lo + cols], s[:, :],
                                     start=False, stop=True).then_inc(t_full, 1)
                    for k2 in range(max(first - 3, 0), last - 3):
                        bank = fill_t(t_at + 3 + k2 - first)
                        for k in range(2):
                            at = slice((2 * k2 + k) * P, (2 * k2 + k + 1) * P)
                            M.matmul(bank[:, k * C:(k + 1) * C], h[:, at], wqkv[l][:, 2 * C:3 * C],
                                     start=True, stop=False)
                            ins = M.matmul(bank[:, k * C:(k + 1) * C], s[:, at], stacked(f"qkv{l}", 2 * C, 3 * C),
                                           start=False, stop=True)
                        ins.then_inc(t_full, 1)
                elif kind == "proj":
                    _, l, b = stage
                    h, s = hT["a"][b], hS["a"][b]
                    turned = turned_at(i)
                    pe.wait_ge(t_free, turned - 1)
                    pe.wait_ge(w_split, 2 if l == 0 else 4)
                    pe.wait_ge(ld_w[l], 16 * (LATE1 if l else LATE0))
                    for k2 in range(NT // 2):
                        bank = fill_s(s_at + k2)
                        for k in range(2):
                            at = slice((2 * k2 + k) * P, (2 * k2 + k + 1) * P)
                            M.matmul(bank[:, k * C:(k + 1) * C], h[:, at], wproj[l][:, :], start=True, stop=False)
                            if k2 == 0 and k == 0:
                                pe.wait_ge(t_free, turned)
                            ins = M.matmul(bank[:, k * C:(k + 1) * C], s[:, at], stacked(f"proj{l}", 0, C),
                                           start=False, stop=True)
                        ins.then_inc(s_full, 1)
                elif kind == "gate":
                    b = stage[1]
                    h, s = hT["b"][b], hS["b"][b]
                    pe.wait_ge(t_free, turned_at(i))
                    bank = fill_s(s_at)
                    for k in range(NT):
                        at = slice(k * P, (k + 1) * P)
                        M.matmul(bank[:, k * E:(k + 1) * E], h[:, at], wgate[:, :], start=True, stop=False)
                        ins = M.matmul(bank[:, k * E:(k + 1) * E], s[:, at], stacked("gate", 0, E),
                                       start=False, stop=True)
                    ins.then_inc(s_full, 1)
                elif kind in ("fc1", "mlp1"):
                    b = stage[1]
                    h, s = hT["b"][b], hS["b"][b]
                    name, w, base = ("w1", w1, CHH * stage[2]) if kind == "fc1" else ("fc1", wfc1, 0)
                    first, last = stage[3:5]
                    pe.wait_ge(w_split, 3 if kind == "fc1" else 4)
                    turned = turned_at(i)
                    pe.wait_ge(t_free, turned - 1)
                    for c in range(first, last):
                        rows = P if kind == "fc1" else min(P, HID - c * P)
                        lo = (base + c) * P
                        bank = fill_t(t_at + c - first)
                        M.matmul(bank[0:rows, :], w[:, lo:lo + rows], h[:, :], start=True, stop=False)
                        if c == first:
                            pe.wait_ge(t_free, turned)
                        M.matmul(bank[0:rows, :], stacked(name, lo, lo + rows), s[:, :], start=False, stop=True)\
                            .then_inc(t_full, 1)
                elif kind in ("fc2", "mlp2"):
                    b = stage[1]
                    first, last = stage[4:6] if kind == "fc2" else (0, NT)
                    for k in range(first, last):
                        bank = fill_s(s_at + k - first)
                        if kind == "fc2":
                            parts = hidden_parts(stage[3])
                        else:
                            parts = [(c, 0, min(P, HID - c * P)) for c in range(CH1)]
                        for c, lo, hi in parts:
                            if k == first:
                                pe.wait_ge(t_free, hidden_made(i, c))
                            if kind == "fc2":
                                chunk = CHH * stage[2] + c
                                w = w2[lo:hi, chunk * C:(chunk + 1) * C]
                            else:
                                w = wfc2[lo:hi, c, :]
                            ins = M.matmul(bank[:, 0:C], hmid[lo:hi, c, k * P:(k + 1) * P], w,
                                           start=(c == parts[0][0]), stop=(c == parts[-1][0]))
                        ins.then_inc(s_full, 1)

                u = unit_of(stage)
                first, last = tiles_of(stage)
                for k4 in range(NT):
                    if u is not None and first <= k4 < last:
                        n, h_ = stage[1] + u // NH, u % NH
                        b = n % B
                        for piece, (lo, _) in enumerate(PIECES[b]):
                            if k4 == 0 and h_ == lo:
                                pe.wait_ge(qk_in[n][piece], 16 * (1 + PARTS))
                        bank = fill_s(s_at + k4 - first)
                        M.matmul(bank[:, :], Qs[b][0:MROW, h_, k4 * P:(k4 + 1) * P], Ks[b][0:MROW, h_, :],
                                 start=True, stop=True).then_inc(s_full, 1)
                    if kind == "slot":
                        _, n0, g, k = stage
                        b, h0 = g // HG, G * (g % HG)
                        if k == 0 and k4 % 2 == 0:
                            pair = (NH * n0 + G * g + k4) // 2
                            pe.wait_ge(m_in[pair % 4], 16 * (pair // 4 + 1))
                        bank = fill_t(t_at + k4)
                        M.matmul(bank[:, :], Ks[b][0:SROWS, h0 + k4, k * P:(k + 1) * P], Qs[b][0:SROWS, h0 + k4, :],
                                 start=True, stop=True).then_inc(t_full, 1)
                if kind == "slot" and (g or k):
                    second(n0, *((g, k - 1) if k else (g - 1, NT - 1)))
                if kind == "tail" and stage[2] == 0:
                    second(stage[1], B * HG - 1, NT - 1)
                pair = turns_pair(stage)
                if pair is not None:
                    pe.wait_ge(m_split, pair + 1)
                    view = fill_t(T_AT[i + 1] - 1)[0:MPARTS * 2 * NT, 0:P // 2].bitcast(BF16)
                    M.transpose(view, mpart[:, pair % 2, :, :].rearrange("p i k -> p (i k)"), identb[:, :])\
                        .then_inc(t_full, 1)
                g, k = finishes(stage)
                if k == 2:
                    gn = HG * stage[1] + g
                    pe.wait_ge(o_copied, gn + 1)
                    bank = fill_s(S_AT[i + 1] - 1)
                    for q in range(NT):
                        ins = M.transpose(bank[:, q * P:(q + 1) * P], oT[:, gn % 2, q * P:(q + 1) * P], ident[:, :])
                    ins.then_inc(s_full, 1)


def kernel(**inputs):
    import numpy as _np
    import concourse.bacc as _bacc
    from concourse import mybir as _mybir
    from concourse.bass_utils import run_bass_kernel_spmd as _run

    nc = _bacc.Bacc("TRN2", target_bir_lowering=False, num_devices=1)
    arrays, args = {}, {}
    for name, value in inputs.items():
        a = _np.ascontiguousarray(value)
        arrays[f"in_{name}_dram"] = a
        args[name] = nc.dram_tensor(f"in_{name}_dram", a.shape, _mybir.dt.from_np(a.dtype),
                                    kind="ExternalInput").ap()
    out = nc.dram_tensor("out_0_dram", (B, N, C), F32, kind="ExternalOutput").ap()
    build(nc, args, out)
    r = _run(nc, [arrays], core_ids=[0])
    return r.results[0]["out_0_dram"]
```
